# Optimizing a Trainium2 kernel written in Bass

```python
import numpy as np
import jax
import jax.numpy as jnp

def _softmax(x, axis=-1):
    return jax.nn.softmax(x, axis=axis)
def _gelu(x):
    return jax.nn.gelu(x, approximate=True)
def _silu(x):
    return jax.nn.silu(x)
def _sigmoid(x):
    return jax.nn.sigmoid(x)
def _layernorm(x, axis=-1, eps=1e-5):
    m = jnp.mean(x, axis=axis, keepdims=True)
    v = jnp.var(x, axis=axis, keepdims=True)
    return (x - m) / jnp.sqrt(v + eps)
def _scatter_add(tgt, idx, src, axis=0):
    return tgt.at[idx].add(src)
def _segment_sum(src, seg, n):
    return jax.ops.segment_sum(src, seg, n)

kernel_name = 'mk_conv_seq_d1_conv_nhwc128_78db3b'

def setup_inputs(seed: int = 0):
    np.random.seed(seed)
    _w = jnp.asarray
    def _rec_inputs():
        import jax
        import jax.numpy as jnp
        _gk = jax.random.key(seed)
        x = -0.0003957 + 1 * jax.random.normal(jax.random.fold_in(_gk, 1), (32, 56, 56, 128), jnp.float32)
        return x
    x = _rec_inputs()
    def _L0_conv_setup():
        import jax, jax.numpy as jnp
        import numpy as np
        B, H, W, C = (32, 56, 56, 128)
        WS, SS, NH = (7, 3, 4)
        HD = C // NH
        N = WS * WS
        NW = H // WS * (W // WS)

        def _rel_index():
            coords = np.stack(np.meshgrid(np.arange(WS), np.arange(WS), indexing='ij'))
            coords = coords.reshape(2, -1)
            rel = coords[:, :, None] - coords[:, None, :]
            rel = rel.transpose(1, 2, 0) + WS - 1
            rel[:, :, 0] *= 2 * WS - 1
            return rel.sum(-1)
        REL_IDX = jnp.asarray(_rel_index())

        def _attn_mask():
            img = np.zeros((H, W))
            cnt = 0
            for h in (slice(0, -WS), slice(-WS, -SS), slice(-SS, None)):
                for w in (slice(0, -WS), slice(-WS, -SS), slice(-SS, None)):
                    img[h, w] = cnt
                    cnt += 1
            mw = img.reshape(H // WS, WS, W // WS, WS).transpose(0, 2, 1, 3).reshape(-1, N)
            diff = mw[:, None, :] - mw[:, :, None]
            return jnp.asarray(np.where(diff != 0, -100.0, 0.0).astype(np.float32))
        MASK = _attn_mask()

        def _ln(x, g, b):
            mu = x.mean(-1, keepdims=True)
            var = x.var(-1, keepdims=True)
            return (x - mu) * jax.lax.rsqrt(var + 1e-05) * g + b

        def _win_part(x):
            x = x.reshape(B, H // WS, WS, W // WS, WS, C)
            return x.transpose(0, 1, 3, 2, 4, 5).reshape(-1, N, C)

        def _win_rev(w):
            x = w.reshape(B, H // WS, W // WS, WS, WS, C)
            return x.transpose(0, 1, 3, 2, 4, 5).reshape(B, H, W, C)
        key = jax.random.key(seed)
        ks = jax.random.split(key, 8)
        s = 0.02
        f = lambda k, shp: jax.random.normal(k, shp, jnp.float32) * s
        return {'x': jax.random.normal(ks[0], (B, H, W, C), jnp.float32), 'g1': jnp.ones((C,), jnp.float32), 'b1': jnp.zeros((C,), jnp.float32), 'w_qkv': f(ks[1], (C, 3 * C)), 'b_qkv': jnp.zeros((3 * C,), jnp.float32), 'w_proj': f(ks[2], (C, C)), 'b_proj': jnp.zeros((C,), jnp.float32), 'rel_table': f(ks[3], ((2 * WS - 1) ** 2, NH)), 'g2': jnp.ones((C,), jnp.float32), 'b2': jnp.zeros((C,), jnp.float32), 'w_fc1': f(ks[4], (C, 4 * C)), 'b_fc1': jnp.zeros((4 * C,), jnp.float32), 'w_fc2': f(ks[5], (4 * C, C)), 'b_fc2': jnp.zeros((C,), jnp.float32)}
    _L0_conv_all = _L0_conv_setup()
    _L0_conv_in = {k: v for k, v in _L0_conv_all.items() if k in ('g1', 'b1', 'w_qkv', 'b_qkv', 'w_proj', 'b_proj', 'rel_table', 'g2', 'b2', 'w_fc1', 'b_fc1', 'w_fc2', 'b_fc2', )}
    del _L0_conv_all

    return {
        "x": x,
        "L0_conv_g1": _L0_conv_in["g1"],
        "L0_conv_b1": _L0_conv_in["b1"],
        "L0_conv_w_qkv": _L0_conv_in["w_qkv"],
        "L0_conv_b_qkv": _L0_conv_in["b_qkv"],
        "L0_conv_w_proj": _L0_conv_in["w_proj"],
        "L0_conv_b_proj": _L0_conv_in["b_proj"],
        "L0_conv_rel_table": _L0_conv_in["rel_table"],
        "L0_conv_g2": _L0_conv_in["g2"],
        "L0_conv_b2": _L0_conv_in["b2"],
        "L0_conv_w_fc1": _L0_conv_in["w_fc1"],
        "L0_conv_b_fc1": _L0_conv_in["b_fc1"],
        "L0_conv_w_fc2": _L0_conv_in["w_fc2"],
        "L0_conv_b_fc2": _L0_conv_in["b_fc2"],
    }

def reference(x, L0_conv_g1, L0_conv_b1, L0_conv_w_qkv, L0_conv_b_qkv, L0_conv_w_proj, L0_conv_b_proj, L0_conv_rel_table, L0_conv_g2, L0_conv_b2, L0_conv_w_fc1, L0_conv_b_fc1, L0_conv_w_fc2, L0_conv_b_fc2):
    import jax
    import jax.numpy as jnp
    def _L0_conv_ref(x, g1, b1, w_qkv, b_qkv, w_proj, b_proj, rel_table, g2, b2, w_fc1, b_fc1, w_fc2, b_fc2):
        import jax, jax.numpy as jnp
        import numpy as np
        B, H, W, C = (32, 56, 56, 128)
        WS, SS, NH = (7, 3, 4)
        HD = C // NH
        N = WS * WS
        NW = H // WS * (W // WS)

        def _rel_index():
            coords = np.stack(np.meshgrid(np.arange(WS), np.arange(WS), indexing='ij'))
            coords = coords.reshape(2, -1)
            rel = coords[:, :, None] - coords[:, None, :]
            rel = rel.transpose(1, 2, 0) + WS - 1
            rel[:, :, 0] *= 2 * WS - 1
            return rel.sum(-1)
        REL_IDX = jnp.asarray(_rel_index())

        def _attn_mask():
            img = np.zeros((H, W))
            cnt = 0
            for h in (slice(0, -WS), slice(-WS, -SS), slice(-SS, None)):
                for w in (slice(0, -WS), slice(-WS, -SS), slice(-SS, None)):
                    img[h, w] = cnt
                    cnt += 1
            mw = img.reshape(H // WS, WS, W // WS, WS).transpose(0, 2, 1, 3).reshape(-1, N)
            diff = mw[:, None, :] - mw[:, :, None]
            return jnp.asarray(np.where(diff != 0, -100.0, 0.0).astype(np.float32))
        MASK = _attn_mask()

        def _ln(x, g, b):
            mu = x.mean(-1, keepdims=True)
            var = x.var(-1, keepdims=True)
            return (x - mu) * jax.lax.rsqrt(var + 1e-05) * g + b

        def _win_part(x):
            x = x.reshape(B, H // WS, WS, W // WS, WS, C)
            return x.transpose(0, 1, 3, 2, 4, 5).reshape(-1, N, C)

        def _win_rev(w):
            x = w.reshape(B, H // WS, W // WS, WS, WS, C)
            return x.transpose(0, 1, 3, 2, 4, 5).reshape(B, H, W, C)
        shortcut = x
        h = _ln(x, g1, b1)
        h = jnp.roll(h, (-SS, -SS), axis=(1, 2))
        xw = _win_part(h)
        qkv = xw @ w_qkv + b_qkv
        q, k, v = [t.reshape(-1, N, NH, HD).transpose(0, 2, 1, 3) for t in jnp.split(qkv, 3, axis=-1)]
        attn = jnp.einsum('whnd,whmd->whnm', q * HD ** (-0.5), k)
        bias = rel_table[REL_IDX].transpose(2, 0, 1)
        attn = attn + bias[None]
        attn = attn.reshape(B, NW, NH, N, N) + MASK[None, :, None]
        attn = jax.nn.softmax(attn.reshape(-1, NH, N, N), axis=-1)
        out = jnp.einsum('whnm,whmd->whnd', attn, v)
        out = out.transpose(0, 2, 1, 3).reshape(-1, N, C) @ w_proj + b_proj
        h = _win_rev(out)
        h = jnp.roll(h, (SS, SS), axis=(1, 2))
        x = shortcut + h
        h2 = _ln(x, g2, b2)
        h2 = jax.nn.gelu(h2 @ w_fc1 + b_fc1, approximate=False) @ w_fc2 + b_fc2
        return x + h2

    def _gn(v, G=32, eps=1e-5):
        B_, H_, W_, C_ = v.shape
        g = v.reshape(B_, H_, W_, G, C_ // G)
        m = jnp.mean(g, axis=(1, 2, 4), keepdims=True)
        s = jnp.var(g, axis=(1, 2, 4), keepdims=True)
        return ((g - m) / jnp.sqrt(s + eps)).reshape(v.shape)

    def _ln_c(v, eps=1e-6):
        m = jnp.mean(v, axis=-1, keepdims=True)
        s = jnp.var(v, axis=-1, keepdims=True)
        return (v - m) / jnp.sqrt(s + eps)

    def _ln_t(v, eps=1e-5):
        m = jnp.mean(v, axis=-1, keepdims=True)
        s = jnp.var(v, axis=-1, keepdims=True)
        return (v - m) / jnp.sqrt(s + eps)

    def _to_tokens(v):
        B_, H_, W_, C_ = v.shape
        return v.reshape(B_, H_ * W_, C_)
    def _from_tokens(t, like):
        return t.reshape(like.shape)

    x = _L0_conv_ref(x, L0_conv_g1, L0_conv_b1, L0_conv_w_qkv, L0_conv_b_qkv, L0_conv_w_proj, L0_conv_b_proj, L0_conv_rel_table, L0_conv_g2, L0_conv_b2, L0_conv_w_fc1, L0_conv_b_fc1, L0_conv_w_fc2, L0_conv_b_fc2)
    return x


_drawn_inputs = setup_inputs


def setup_inputs(seed=0):
    import zlib

    import numpy as np

    out = dict(_drawn_inputs(seed))
    spreads = {'L0_conv_g1': (1.0, 0.6),
     'L0_conv_b1': (0.0, 0.8),
     'L0_conv_b_qkv': (0.0, 0.411),
     'L0_conv_b_proj': (0.0, 0.1),
     'L0_conv_g2': (1.0, 0.6),
     'L0_conv_b2': (0.0, 0.8),
     'L0_conv_b_fc1': (0.0, 0.323),
     'L0_conv_b_fc2': (0.0, 0.1)}
    factors = {'L0_conv_w_qkv': 5.636, 'L0_conv_rel_table': 27.231}
    for name, (base, spread) in spreads.items():
        noise = np.random.default_rng([zlib.crc32(name.encode()), seed]).standard_normal(out[name].shape)
        drawn = base * np.exp(spread * noise) if base else spread * noise
        out[name] = jnp.asarray(drawn.astype(out[name].dtype))
    for name, factor in factors.items():
        out[name] = (out[name] * factor).astype(out[name].dtype)
    return out
```

```python
from contextlib import ExitStack

import numpy as np

import concourse.bass as bass
from concourse import mybir

F32 = mybir.dt.float32
ALU = mybir.AluOpType
ACT = mybir.ActivationFunctionType
AX_X = mybir.AxisListType.X

ROWS = COLS = 56
C = 128
HEADS = 4
HD = C // HEADS
WIN = 7
SHIFT = 3
N = WIN * WIN
HIDDEN = 4 * C
CHUNKS = HIDDEN // C
WINDOWS = COLS // WIN
PAIRS = WINDOWS // 2
HALF = 64
BANDS = 2
BAND = WINDOWS * N
STEP_ROWS = BANDS * WIN
STEPS = ROWS // STEP_ROWS
TOK = BANDS * COLS
TILES = WIN
STEP = TILES * TOK
IMG = ROWS * COLS
WHOLE = WINDOWS - 1
HEAD = WIN - SHIFT
FIRST = 4
HALVES = ((0, FIRST), (FIRST, TILES))
LOADS = [2, 2, 2, 3]
SCALE = float(HD) ** -0.5
EPS = 1e-5

PER_QKVO = 8
O_USE = (0, 1)
Q_USE, K_USE, V_USE = (2, 5), (3, 6), (4, 7)
BEFORE_STEP_0 = 6


class At:

    def __init__(self, img, s, attn=True, nxt=True, mlp=True):
        self.img, self.s = img, s
        self.attn, self.nxt, self.mlp = attn, nxt, mlp

    def count(self, per, k, d=0):
        return self.img * (STEPS * per) + ((self.s + d) * per + k)

    def slot(self, d=0):
        return (self.s + d) % STEPS

    def image(self, d=0):
        return self.img + (self.s + d) // STEPS


def wait(eng, sem, value):
    if isinstance(value, int) and value <= 0:
        return
    eng.wait_ge(sem, value)


def run_steps(eng, images, step):
    step(At(-1, STEPS - 1, attn=False, mlp=False))
    for s in range(STEPS):
        step(At(0, s, mlp=s > 0))
    if images > 2:
        with eng.Fori(1, images - 1) as img:
            for s in range(STEPS):
                step(At(img, s))
    for s in range(STEPS):
        step(At(images - 1, s, nxt=s < STEPS - 1))
    step(At(images, 0, attn=False, nxt=False))


def swin_block(nc, x, g1, b1, w_qkv, b_qkv, w_proj, b_proj, rel_flipped, g2, b2, w_fc1, b_fc1, w_fc2,
               b_fc2, mask, out):
    images = x.shape[0]

    with ExitStack() as ctx:
        def sb(name, shape, dt=F32):
            return ctx.enter_context(nc.sbuf_tensor(name, shape, dt))

        def sem(name):
            return ctx.enter_context(nc.semaphore(name))

        x_in = sb("x_in", [TOK, STEPS, TILES, C])
        stream = sb("stream", [TOK, STEPS, TILES, C])
        xn1 = sb("xn1", [TOK, TILES, C])
        xn2 = sb("xn2", [TOK, TILES, C])
        raw1 = sb("raw1", [TOK, TILES, 6])
        raw2 = sb("raw2", [TOK, TILES, 6])
        part1 = sb("part1", [TOK, 4, TILES])
        part2 = sb("part2", [TOK, 4, TILES])
        mean1 = sb("mean1", [TOK, TILES])
        mean2 = sb("mean2", [TOK, TILES])
        ve1 = sb("ve1", [TOK, TILES])
        ve2 = sb("ve2", [TOK, TILES])
        rstd1 = sb("rstd1", [TOK, TILES])
        rstd2 = sb("rstd2", [TOK, TILES])
        xT = sb("xT", [C, BANDS, WINDOWS, N])
        qT = sb("qT", [C, BANDS, BAND])
        kT = sb("kT", [C, BANDS, BAND])
        oT = sb("oT", [C, TILES, BANDS, COLS])
        x2T = sb("x2T", [C, STEP])
        hT = sb("hT", [C, CHUNKS, STEP])
        scores = sb("scores", [128, BANDS, HEADS, PAIRS, N])
        row_max = sb("row_max", [128, BANDS, HEADS, PAIRS])
        row_sum = sb("row_sum", [128, BANDS, PAIRS, HEADS])
        row_inv = sb("row_inv", [128, BANDS, PAIRS, HEADS])
        probs = sb("probs", [128, BANDS, PAIRS, HEADS, HALF])
        probsT = sb("probsT", [128, BANDS, PAIRS, 2, 128])
        vd = sb("vd", [128, BANDS, WINDOWS, 2, 2, HD])
        wqkv = sb("wqkv", [C, 3 * C])
        wq = sb("wq", [C, C])
        wk = sb("wk", [C, C])
        wv = sb("wv", [C, 2, 2, HD])
        wproj = sb("wproj", [C, C])
        wfc1_raw = sb("wfc1_raw", [C, HIDDEN])
        wfc1 = sb("wfc1", [C, HIDDEN])
        wfc2 = sb("wfc2", [C, CHUNKS, C])
        vecs = sb("vecs", [C, 4])
        bqkv = sb("bqkv", [C, 3])
        bfc1 = sb("bfc1", [C, CHUNKS])
        bias_q = sb("bias_q", [C, 1])
        bias_k = sb("bias_k", [C, 1])
        bias_v = sb("bias_v", [C, 1])
        bias_v_wide = sb("bias_v_wide", [C, TOK])
        bias_h = sb("bias_h", [C, CHUNKS])
        brow_proj_in = sb("brow_proj_in", [TOK, C])
        brow_proj = sb("brow_proj", [TOK, C])
        brow_fc2 = sb("brow_fc2", [TOK, C])
        rel = sb("rel", [128, HEADS, N])
        mask_sb = sb("mask_sb", [128, 2, PAIRS, N])
        bias_rel = sb("bias_rel", [128, 2, HEADS, PAIRS, N])
        minus_half = sb("minus_half", [TOK, TILES])
        ident = sb("ident", [128, 128])

        psum = ctx.enter_context(nc.psum_tensor("psum", [128, 8, 512], F32))
        S_BANK, QKVO_BANK, TOK_BANK = 0, 4, 6

        weights_loaded = sem("weights_loaded")
        rel_cleared = sem("rel_cleared")
        rel_loaded = sem("rel_loaded")
        ident_zeroed = sem("ident_zeroed")
        ident_ready = sem("ident_ready")
        weights_ready = sem("weights_ready")
        bias_products = sem("bias_products")
        bias_v_ready = sem("bias_v_ready")
        brow_product = sem("brow_product")
        consts_ready = sem("consts_ready")
        x_loaded = [sem(f"x_loaded{i}") for i in range(STEPS)]
        out_stored = [sem(f"out_stored{i}") for i in range(STEPS)]
        raw1_done = sem("raw1_done")
        parts1_done = sem("parts1_done")
        stats1_done = sem("stats1_done")
        var1_ready = sem("var1_ready")
        xn1_ready = sem("xn1_ready")
        scores_biased = sem("scores_biased")
        max_done = sem("max_done")
        scores_shifted = sem("scores_shifted")
        sum_done = sem("sum_done")
        inv_ready = sem("inv_ready")
        residual_added = sem("residual_added")
        raw2_done = sem("raw2_done")
        parts2_done = sem("parts2_done")
        stats2_done = sem("stats2_done")
        var2_ready = sem("var2_ready")
        xn2_ready = sem("xn2_ready")
        out_added = sem("out_added")
        x_biased = sem("x_biased")
        rstd1_ready = sem("rstd1_ready")
        probs_normed = sem("probs_normed")
        rstd2_ready = sem("rstd2_ready")
        x1_biased = sem("x1_biased")
        xT_made = sem("xT_made")
        qkvo_made = sem("qkvo_made")
        scores_made = sem("scores_made")
        probsT_made = sem("probsT_made")
        proj_made = sem("proj_made")
        x2T_made = sem("x2T_made")
        fc1_made = sem("fc1_made")
        fc2_made = sem("fc2_made")
        xT_copied = sem("xT_copied")
        qkvo_copied = sem("qkvo_copied")
        exp_done = sem("exp_done")
        probsT_copied = sem("probsT_copied")
        x2T_copied = sem("x2T_copied")
        gelu_done = sem("gelu_done")

        def qkvo_psum(use):
            return psum[:, QKVO_BANK + use % 2, :]

        def tok_psum(use):
            return psum[:, TOK_BANK + use % 2, :]

        def qkvo_count(at, use, d=0):
            return at.count(PER_QKVO, BEFORE_STEP_0 + use + 1, d)

        X2T, FC1, FC2A, XT, FC2B, PROJ = 0, 2, 10, 11, 13, 14

        def token_pieces(s, dram, img, tile):
            pieces = []
            for band in range(BANDS):
                row = STEP_ROWS * s + WIN * band + SHIFT
                whole = min(WIN, ROWS - row)
                for first, t0, t1 in ((row, 0, whole), (0, whole, WIN)):
                    if t0 < t1:
                        rows = dram[img, first * COLS:(first + t1 - t0) * COLS, :]
                        pieces.append((rows.rearrange("(t p) c -> p t c", p=COLS),
                                       tile[COLS * band:COLS * (band + 1), t0:t1, :]))
            assert len(pieces) == LOADS[s]
            return pieces

        def dma_count(s, img):
            return img * (16 * LOADS[s]) + 16 * LOADS[s]

        block = ctx.enter_context(nc.Block())

        @block.sync
        def _(sp):
            def load(img, s):
                for src, dst in token_pieces(s, x, img, x_in[:, s, :, :]):
                    sp.dma_start(dst, src).then_inc(x_loaded[s], 16)

            def store(img, s):
                for dst, src in token_pieces(s, out, img, stream[:, s, :, :]):
                    sp.dma_start(dst, src).then_inc(out_stored[s], 16)

            load(0, 0)
            for dst, src in ((wqkv[:, :], w_qkv), (vecs[:, 0:1], g1), (vecs[:, 1:2], b1), (vecs[:, 2:3], g2),
                             (vecs[:, 3:4], b2), (bqkv[:, :], b_qkv), (wproj[:, :], w_proj),
                             (wfc1_raw[:, :], w_fc1), (bfc1[:, :], b_fc1),
                             (wfc2[:, :, :], w_fc2.rearrange("(k p) n -> p k n", p=C)),
                             (brow_proj_in[:, :], b_proj.to_broadcast([TOK, C])),
                             (brow_fc2[:, :], b_fc2.to_broadcast([TOK, C])),
                             (mask_sb[:, :, :, :], mask)):
                sp.dma_start(dst, src).then_inc(weights_loaded, 16)
            for s in range(1, STEPS):
                load(0, s)

            def step(at):
                if at.attn and not (isinstance(at.img, int) and at.img == images - 1):
                    wait(sp, xn1_ready, at.count(1, 1))
                    wait(sp, x_biased, at.count(1, 1))
                    load(at.image(STEPS), at.slot())
                if at.mlp:
                    wait(sp, out_added, at.count(2, 2, -1))
                    store(at.image(-1), at.slot(-1))

            run_steps(sp, images, step)
            for s in range(STEPS):
                sp.wait_ge(out_stored[s], dma_count(s, images - 1))

        @block.gpsimd
        def _(pool):
            pool.memset(ident[:, :], 0.0).then_inc(ident_zeroed, 1)
            pool.wait_ge(ident_zeroed, 1)
            pool.affine_select(out=ident[:, :], in_=ident[:, :], compare_op=ALU.not_equal, fill=1.0, base=0,
                               pattern=[[-1, 128]], channel_multiplier=1).then_inc(ident_ready, 1)
            pool.wait_ge(rel_cleared, 1)
            for half in range(2):
                for ni in range(WIN):
                    for nj in range(WIN):
                        p = HALF * half + WIN * ni + nj
                        i0, j0 = WIN - 1 - ni, WIN - 1 - nj
                        pool.dma_start(rel[p:p + 1, :, :].rearrange("p h (i j) -> p h i j", i=WIN),
                                       rel_flipped[:, :, i0:i0 + WIN, j0:j0 + WIN]).then_inc(rel_loaded, 16)
            pool.memset(minus_half[:, :], -0.5).then_inc(consts_ready, 1)
            pool.wait_ge(consts_ready, 2)
            pool.wait_ge(weights_loaded, 13 * 16)

            def step(at):
                if at.nxt:
                    wait(pool, x_loaded[at.slot(1)], dma_count(at.slot(1), at.image(1)))
                    before = at.image(1) - 1
                    wait(pool, out_stored[at.slot(1)],
                         0 if isinstance(before, int) and before < 0 else dma_count(at.slot(1), before))
                    pool.tensor_tensor(stream[:, at.slot(1), :, :], x_in[:, at.slot(1), :, :],
                                       brow_proj[:, :].unsqueeze(1).to_broadcast([TOK, TILES, C]),
                                       ALU.add).then_inc(x_biased, 1)
                    wait(pool, var1_ready, at.count(1, 1, 1))
                    pool.tensor_tensor(rstd1[:, :], ve1[:, :], minus_half[:, :], ALU.pow).then_inc(rstd1_ready, 1)
                if at.attn:
                    for band in range(BANDS):
                        wait(pool, inv_ready, at.count(2, band + 1))
                        p = probs[:, band, :, :, 0:N].rearrange("p a h m -> p (a h) m")
                        r = row_inv[:, band, :, :].rearrange("p a h -> p (a h)")
                        pool.tensor_tensor(p, p, r.unsqueeze(2).to_broadcast([128, PAIRS * HEADS, N]),
                                           ALU.mult).then_inc(probs_normed, 1)
                    wait(pool, var2_ready, at.count(1, 1))
                    pool.tensor_tensor(rstd2[:, :], ve2[:, :], minus_half[:, :], ALU.pow).then_inc(rstd2_ready, 1)
                    wait(pool, xn2_ready, at.count(1, 1))
                    pool.tensor_tensor(stream[:, at.slot(), :, :], stream[:, at.slot(), :, :],
                                       brow_fc2[:, :].unsqueeze(1).to_broadcast([TOK, TILES, C]),
                                       ALU.add).then_inc(x1_biased, 1)

            run_steps(pool, images, step)

        @block.scalar
        def _(act):
            act.wait_ge(weights_ready, 1)
            act.wait_ge(consts_ready, 2)

            def columns_shifted(image, windows, copy):
                last = windows[:, WHOLE, :, :]
                copy(image[:, :, SHIFT:SHIFT + WHOLE * WIN].rearrange("c i (w j) -> c w i j", j=WIN),
                     windows[:, 0:WHOLE, :, :])
                copy(image[:, :, COLS - HEAD:COLS], last[:, :, 0:HEAD])
                return copy(image[:, :, 0:SHIFT], last[:, :, HEAD:WIN])

            def exp(at, band):
                wait(act, scores_shifted, at.count(2, band + 1))
                wait(act, probsT_made, at.count(4, 2 * band + 2, -1))
                act.activation(probs[:, band, :, :, 0:N].rearrange("p a h m -> p h a m"),
                               scores[:, band, :, :, :], ACT.Exp).then_inc(exp_done, 1)

            def copy_probsT(at, band):
                for f in range(2):
                    wait(act, probsT_made, at.count(4, 2 * band + f + 1))
                    act.activation(probsT[:, band, 2 * f:2 * f + 2, :, :].rearrange("p a q n -> p (a q n)"),
                                   psum[:, S_BANK + 2 * band + f, :], ACT.Copy).then_inc(probsT_copied, 1)

            def copy_o(at, band):
                use = O_USE[band]
                wait(act, qkvo_made, qkvo_count(at, use))
                windows = qkvo_psum(use)[:, 0:BAND].rearrange("c (w i j) -> c w i j", i=WIN, j=WIN)
                columns_shifted(oT[:, :, band, :], windows,
                                lambda image, win: act.activation(image, win, ACT.Copy)).then_inc(qkvo_copied, 1)

            def copy_x(h):
                t0, t1 = HALVES[h]
                for band in range(BANDS):
                    rows = tok_psum(XT + h)[:, 0:(t1 - t0) * TOK].rearrange("c (t b j) -> c t b j", b=BANDS, j=COLS)
                    windows = xT[:, band, :, :].rearrange("c w (i j) -> c w i j", j=WIN)
                    last = columns_shifted(rows[:, :, band, :], windows[:, :, t0:t1, :],
                                           lambda image, win: act.activation(win, image, ACT.Copy))
                return last

            def copy_qkv(at, band):
                for use, dst, bias in ((Q_USE[band], qT, bias_q), (K_USE[band], kT, bias_k)):
                    wait(act, qkvo_made, qkvo_count(at, use))
                    act.activation(dst[:, band, :], qkvo_psum(use)[:, 0:BAND], ACT.Identity,
                                   bias=bias[:, :]).then_inc(qkvo_copied, 1)
                use = V_USE[band]
                wait(act, qkvo_made, qkvo_count(at, use))
                for hp in range(2):
                    p = slice(HALF * hp, HALF * hp + N)
                    v = qkvo_psum(use)[p, :].rearrange("m (w q d) -> m w q d", w=WINDOWS, q=2)
                    last = act.activation(vd[p, band, :, :, hp, :], v, ACT.Copy)
                last.then_inc(qkvo_copied, 1)

            def step(at):
                if at.attn:
                    exp(at, 0)
                if at.mlp:
                    for h, (t0, t1) in enumerate(HALVES):
                        wait(act, x2T_made, at.count(2, h + 1, -1))
                        act.activation(x2T[:, t0 * TOK:t1 * TOK], tok_psum(X2T + h)[:, 0:(t1 - t0) * TOK],
                                       ACT.Copy).then_inc(x2T_copied, 1)
                    for n in range(BANDS * CHUNKS):
                        band, chunk = divmod(n, CHUNKS)
                        wait(act, fc1_made, at.count(BANDS * CHUNKS, n + 1, -1))
                        act.activation(hT[:, chunk, band * BAND:(band + 1) * BAND], tok_psum(FC1 + n)[:, 0:BAND],
                                       ACT.Gelu, bias=bias_h[:, chunk:chunk + 1]).then_inc(gelu_done, 1)
                if at.attn:
                    exp(at, 1)
                    copy_probsT(at, 0)
                    copy_o(at, 0)
                    copy_probsT(at, 1)
                if at.nxt:
                    for h in range(2):
                        wait(act, xT_made, at.count(2, h + 1, 1))
                        copy_x(h).then_inc(xT_copied, 1)
                if at.attn:
                    copy_o(at, 1)
                if at.nxt:
                    copy_qkv(at, 0)
                    copy_qkv(at, 1)

            run_steps(act, images, step)

        @block.vector
        def _(dve):
            dve.memset(rel[:, :, :], 0.0).then_inc(rel_cleared, 1)
            dve.memset(probs[:, :, :, :, :], 0.0)
            dve.memset(vd[:, :, :, :, :, :], 0.0)
            dve.memset(psum[:, 0:4, :], 0.0).then_inc(weights_ready, 1)
            dve.wait_ge(weights_loaded, 13 * 16)
            dve.tensor_scalar(wq[:, :], wqkv[:, 0:C], vecs[:, 0:1], SCALE, ALU.mult, ALU.mult)
            dve.tensor_scalar(wk[:, :], wqkv[:, C:2 * C], vecs[:, 0:1], None, ALU.mult)
            dve.tensor_scalar(wv[:, :, :, :].rearrange("c p q d -> c q p d"),
                              wqkv[:, 2 * C:3 * C].rearrange("c (q p d) -> c q p d", q=2, p=2),
                              vecs[:, 0:1], None, ALU.mult)
            dve.tensor_scalar(wfc1[:, :], wfc1_raw[:, :], vecs[:, 2:3], None, ALU.mult).then_inc(weights_ready, 1)
            dve.wait_ge(bias_products, 1)
            made = psum[:, QKVO_BANK, :]
            dve.tensor_scalar(bias_q[:, :], made[:, 0:1], bqkv[:, 0:1], SCALE, ALU.add, ALU.mult)
            dve.tensor_tensor(bias_k[:, :], made[:, 1:2], bqkv[:, 1:2], ALU.add)
            dve.tensor_tensor(bias_v[:, :], made[:, 2:3], bqkv[:, 2:3], ALU.add)
            dve.tensor_tensor(bias_h[:, :], made[:, 3:3 + CHUNKS], bfc1[:, :], ALU.add).then_inc(bias_v_ready, 1)
            dve.wait_ge(bias_v_ready, 1)
            dve.tensor_copy(bias_v_wide[:, :], bias_v[:, 0:1].to_broadcast([C, TOK])).then_inc(bias_v_ready, 1)
            dve.wait_ge(brow_product, 1)
            dve.tensor_tensor(brow_proj[:, :], psum[0:TOK, QKVO_BANK + 1, 0:C], brow_proj_in[:, :], ALU.add)
            dve.wait_ge(rel_loaded, 2 * N * 16)
            for last_band in range(2):
                for h in range(HEADS):
                    last = dve.tensor_tensor(bias_rel[:, last_band, h, :, :], mask_sb[:, last_band, :, :],
                                             rel[:, h, :].unsqueeze(1).to_broadcast([128, PAIRS, N]), ALU.add)
            last.then_inc(consts_ready, 1)
            dve.wait_ge(consts_ready, 2)

            def raw_stats(src, raw, done):
                for t in range(TILES):
                    last = dve.bn_stats(raw[:, t, :], src[:, t, :])
                last.then_inc(done, 1)

            def mean_var(raw, part, mean, ve, raw_done, parts_done, stats_done, ready, n):
                mean0, mean1 = raw[:, :, 1], raw[:, :, 4]
                wait(dve, raw_done, n)
                dve.tensor_tensor(part[:, 0, :], mean0, mean1, ALU.add)
                dve.tensor_tensor(part[:, 1, :], mean0, mean1, ALU.subtract)
                dve.scalar_tensor_tensor(part[:, 2, :], raw[:, :, 2], C * EPS, raw[:, :, 5], ALU.add,
                                         ALU.add).then_inc(parts_done, 1)
                wait(dve, parts_done, n)
                dve.tensor_scalar(mean[:, :], part[:, 0, :], 0.5, None, ALU.mult)
                dve.scalar_tensor_tensor(part[:, 3, :], part[:, 1, :], 0.25, part[:, 1, :], ALU.mult,
                                         ALU.mult).then_inc(stats_done, 1)
                wait(dve, stats_done, n)
                dve.scalar_tensor_tensor(ve[:, :], part[:, 2, :], 1.0 / C, part[:, 3, :], ALU.mult,
                                         ALU.add).then_inc(ready, 1)

            def normalise(dst, src, mean, rstd, ready):
                for t in range(TILES):
                    last = dve.tensor_scalar(dst[:, t, :], src[:, t, :], mean[:, t:t + 1], rstd[:, t:t + 1],
                                             ALU.subtract, ALU.mult)
                last.then_inc(ready, 1)

            def shift_scores(at, band):
                sc = scores[:, band, :, :, :].rearrange("p h a m -> p h (a m)")
                rows = scores[:, band, :, :, :].rearrange("p h a m -> p (h a) m")
                mx = row_max[:, band, :, :].rearrange("p h a -> p (h a)")
                last_band = int(at.s == STEPS - 1 and band == BANDS - 1)
                wait(dve, scores_made, at.count(2, band + 1))
                wait(dve, exp_done, at.count(2, band + 1, -1))
                dve.tensor_tensor(sc, psum[:, S_BANK:S_BANK + HEADS, 0:PAIRS * N],
                                  bias_rel[:, last_band, :, :, :].rearrange("p h a m -> p h (a m)"),
                                  ALU.add).then_inc(scores_biased, 1)
                wait(dve, scores_biased, at.count(2, band + 1))
                dve.tensor_reduce(mx, rows, AX_X, ALU.max).then_inc(max_done, 1)
                wait(dve, max_done, at.count(2, band + 1))
                dve.tensor_tensor(rows, rows, mx.unsqueeze(2).to_broadcast([128, HEADS * PAIRS, N]),
                                  ALU.subtract).then_inc(scores_shifted, 1)

            def inverse_sums(at, band):
                p = probs[:, band, :, :, 0:N].rearrange("p a h m -> p (a h) m")
                s = row_sum[:, band, :, :].rearrange("p a h -> p (a h)")
                r = row_inv[:, band, :, :].rearrange("p a h -> p (a h)")
                wait(dve, exp_done, at.count(2, band + 1))
                dve.tensor_reduce(s, p, AX_X, ALU.add).then_inc(sum_done, 1)
                wait(dve, sum_done, at.count(2, band + 1))
                dve.reciprocal(r, s).then_inc(inv_ready, 1)

            def add_to_stream(slot, use, h):
                t0, t1 = HALVES[h]
                s = stream[:, slot, t0:t1, :].rearrange("p t c -> p (t c)")
                return dve.tensor_tensor(s, tok_psum(use)[0:TOK, 0:(t1 - t0) * C], s, ALU.add)

            def step(at):
                if at.attn:
                    shift_scores(at, 0)
                if at.nxt:
                    wait(dve, x_loaded[at.slot(1)], dma_count(at.slot(1), at.image(1)))
                    wait(dve, xn1_ready, at.count(1, 1))
                    raw_stats(x_in[:, at.slot(1), :, :], raw1, raw1_done)
                    mean_var(raw1, part1, mean1, ve1, raw1_done, parts1_done, stats1_done, var1_ready,
                             at.count(1, 1, 1))
                if at.attn:
                    inverse_sums(at, 0)
                    shift_scores(at, 1)
                if at.nxt:
                    wait(dve, rstd1_ready, at.count(1, 1, 1))
                    wait(dve, xT_made, at.count(2, 2))
                    normalise(xn1, x_in[:, at.slot(1), :, :], mean1, rstd1, xn1_ready)
                if at.attn:
                    inverse_sums(at, 1)
                if at.mlp:
                    wait(dve, x1_biased, at.count(1, 1, -1))
                    for h in range(2):
                        wait(dve, fc2_made, at.count(2, h + 1, -1))
                        add_to_stream(at.slot(-1), (FC2A, FC2B)[h], h).then_inc(out_added, 1)
                if at.attn:
                    wait(dve, x_biased, at.count(1, 1))
                    for h in range(2):
                        wait(dve, proj_made, at.count(2, h + 1))
                        add_to_stream(at.slot(), PROJ + h, h).then_inc(residual_added, 1)
                    wait(dve, residual_added, at.count(2, 2))
                    raw_stats(stream[:, at.slot(), :, :], raw2, raw2_done)
                    mean_var(raw2, part2, mean2, ve2, raw2_done, parts2_done, stats2_done, var2_ready, at.count(1, 1))
                    wait(dve, rstd2_ready, at.count(1, 1))
                    wait(dve, x2T_made, at.count(2, 2, -1))
                    normalise(xn2, stream[:, at.slot(), :, :], mean2, rstd2, xn2_ready)

            run_steps(dve, images, step)

        @block.tensor
        def _(pe):
            pe.wait_ge(weights_loaded, 13 * 16)
            for k in range(3):
                pe.matmul(psum[:, QKVO_BANK, k:k + 1], wqkv[:, k * C:(k + 1) * C], vecs[:, 1:2],
                          start=True, stop=True)
            for k in range(CHUNKS):
                last = pe.matmul(psum[:, QKVO_BANK, 3 + k:4 + k], wfc1_raw[:, k * C:(k + 1) * C], vecs[:, 3:4],
                                 start=True, stop=True)
            last.then_inc(bias_products, 1)
            pe.wait_ge(bias_v_ready, 2)
            pe.matmul(psum[0:TOK, QKVO_BANK + 1, 0:C], bias_v_wide[:, :], wproj[:, :], start=True,
                      stop=True).then_inc(brow_product, 1)
            pe.wait_ge(weights_ready, 2)
            pe.wait_ge(ident_ready, 1)
            pe.wait_ge(consts_ready, 2)

            def make_scores(at, band):
                for pair in range(PAIRS):
                    for w in range(2):
                        cols = slice((2 * pair + w) * N, (2 * pair + w + 1) * N)
                        for h in range(HEADS):
                            rows = slice(HD * h, HD * (h + 1))
                            last = pe.matmul(psum[HALF * w:HALF * w + N, S_BANK + h, pair * N:(pair + 1) * N],
                                             qT[rows, band, cols], kT[rows, band, cols], start=True, stop=True)
                last.then_inc(scores_made, 1)

            def transpose_tiles(src, use, h):
                t0, t1 = HALVES[h]
                for t in range(t0, t1):
                    last = pe.transpose(tok_psum(use)[:, (t - t0) * TOK:(t - t0 + 1) * TOK], src[:, t, :],
                                        ident[0:TOK, 0:TOK])
                return last

            def transpose_probs(at, band):
                wait(pe, scores_biased, at.count(2, 2))
                wait(pe, probs_normed, at.count(2, band + 1))
                for f in range(2):
                    for n in range(4):
                        pair, hq = 2 * f + n // 2, n % 2
                        last = pe.transpose(psum[:, S_BANK + 2 * band + f, 128 * n:128 * (n + 1)],
                                            probs[:, band, pair, 2 * hq:2 * hq + 2, :].rearrange("p h m -> p (h m)"),
                                            ident[:, :])
                    last.then_inc(probsT_made, 1)

            def attend(at, band):
                wait(pe, probsT_copied, at.count(4, 2 * band + 2))
                wait(pe, qkvo_copied, qkvo_count(at, V_USE[band], -1))
                for w in range(WINDOWS):
                    for hq in range(2):
                        last = pe.matmul(qkvo_psum(O_USE[band])[HALF * hq:HALF * (hq + 1), w * N:(w + 1) * N],
                                         vd[:, band, w, hq, :, :].rearrange("m p d -> m (p d)"),
                                         probsT[:, band, w // 2, hq, HALF * (w % 2):HALF * (w % 2) + N],
                                         start=True, stop=True)
                last.then_inc(qkvo_made, 1)

            def make_qkv(at, band):
                wait(pe, xT_copied, at.count(2, 2, 1))
                for use, w in ((Q_USE[band], wq), (K_USE[band], wk)):
                    wait(pe, qkvo_copied, qkvo_count(at, use - 2))
                    pe.matmul(qkvo_psum(use)[:, 0:BAND], w[:, :], xT[:, band, :, :].rearrange("c w n -> c (w n)"),
                              start=True, stop=True).then_inc(qkvo_made, 1)
                use = V_USE[band]
                wait(pe, qkvo_copied, qkvo_count(at, use - 2))
                for w in range(WINDOWS):
                    for hp in range(2):
                        last = pe.matmul(qkvo_psum(use)[HALF * hp:HALF * hp + N, w * HALF:(w + 1) * HALF],
                                         xT[:, band, w, :], wv[:, hp, :, :].rearrange("c q d -> c (q d)"), start=True, stop=True)
                last.then_inc(qkvo_made, 1)

            def project(at, h):
                t0, t1 = HALVES[h]
                for t in range(t0, t1):
                    last = pe.matmul(tok_psum(PROJ + h)[0:TOK, (t - t0) * C:(t - t0 + 1) * C],
                                     oT[:, t, :, :].rearrange("c b j -> c (b j)"), wproj[:, :], start=True, stop=True)
                last.then_inc(proj_made, 1)

            def make_hidden(at, band):
                for n in range(band * CHUNKS, (band + 1) * CHUNKS):
                    if n < 2:
                        wait(pe, x2T_copied, at.count(2, n + 1, -1))
                    else:
                        wait(pe, gelu_done, at.count(BANDS * CHUNKS, n - 1, -1))
                    chunk = n % CHUNKS
                    pe.matmul(tok_psum(FC1 + n)[:, 0:BAND], wfc1[:, chunk * C:(chunk + 1) * C],
                              x2T[:, band * BAND:(band + 1) * BAND], start=True, stop=True).then_inc(fc1_made, 1)

            def make_out(at, use, h):
                t0, t1 = HALVES[h]
                for t in range(t0, t1):
                    for chunk in range(CHUNKS):
                        last = pe.matmul(tok_psum(use)[0:TOK, (t - t0) * C:(t - t0 + 1) * C],
                                         hT[:, chunk, t * TOK:(t + 1) * TOK], wfc2[:, chunk, :],
                                         start=chunk == 0, stop=chunk == CHUNKS - 1)
                last.then_inc(fc2_made, 1)

            def step(at):
                if at.attn:
                    wait(pe, qkvo_copied, qkvo_count(at, K_USE[0], -1))
                    wait(pe, probsT_copied, at.count(4, 4, -1))
                    make_scores(at, 0)
                if at.mlp:
                    wait(pe, xn2_ready, at.count(1, 1, -1))
                    for h in range(2):
                        wait(pe, residual_added, at.count(2, h + 1, -1))
                        transpose_tiles(xn2, X2T + h, h).then_inc(x2T_made, 1)
                if at.attn:
                    wait(pe, qkvo_copied, qkvo_count(at, K_USE[1], -1))
                    wait(pe, scores_biased, at.count(2, 1))
                    make_scores(at, 1)
                if at.mlp:
                    make_hidden(at, 0)
                    make_hidden(at, 1)
                if at.attn:
                    transpose_probs(at, 0)
                if at.mlp:
                    wait(pe, gelu_done, at.count(BANDS * CHUNKS, BANDS * CHUNKS, -1))
                    make_out(at, FC2A, 0)
                if at.attn:
                    attend(at, 0)
                    transpose_probs(at, 1)
                if at.nxt:
                    wait(pe, xn1_ready, at.count(1, 1, 1))
                    transpose_tiles(xn1, XT, 0).then_inc(xT_made, 1)
                    wait(pe, out_added, at.count(2, 1, -1))
                    transpose_tiles(xn1, XT + 1, 1).then_inc(xT_made, 1)
                if at.mlp:
                    if at.nxt:
                        wait(pe, xT_copied, at.count(2, 1, 1))
                    make_out(at, FC2B, 1)
                if at.attn:
                    attend(at, 1)
                if at.nxt:
                    make_qkv(at, 0)
                if at.attn:
                    wait(pe, qkvo_copied, qkvo_count(at, O_USE[1]))
                    if at.nxt:
                        wait(pe, xT_copied, at.count(2, 2, 1))
                    wait(pe, out_added, at.count(2, 1, -1))
                    project(at, 0)
                    wait(pe, out_added, at.count(2, 2, -1))
                    project(at, 1)
                if at.nxt:
                    make_qkv(at, 1)

            run_steps(pe, images, step)


def window_mask():
    part = np.zeros((2, WIN), np.int64)
    part[1, WIN - SHIFT:] = 1
    full = np.zeros((128, 2, PAIRS, N), np.float32)
    for last_band in range(2):
        for w in range(WINDOWS):
            region = (2 * part[last_band][:, None] + part[int(w == WINDOWS - 1)][None, :]).reshape(-1)
            differ = region[:, None] != region[None, :]
            p0 = HALF * (w % 2)
            full[p0:p0 + N, last_band, w // 2, :] = np.where(differ, -100.0, 0.0)
    return full


def kernel(x, L0_conv_g1, L0_conv_b1, L0_conv_w_qkv, L0_conv_b_qkv, L0_conv_w_proj, L0_conv_b_proj,
           L0_conv_rel_table, L0_conv_g2, L0_conv_b2, L0_conv_w_fc1, L0_conv_b_fc1, L0_conv_w_fc2,
           L0_conv_b_fc2):
    import concourse.bacc as bacc
    from concourse.bass_utils import run_bass_kernel_spmd

    x = np.asarray(x)
    shape = x.shape
    span = 2 * WIN - 1
    laid = {
        "x": x.reshape(shape[0], IMG, C),
        "g1": np.asarray(L0_conv_g1).reshape(C, 1),
        "b1": np.asarray(L0_conv_b1).reshape(C, 1),
        "w_qkv": np.asarray(L0_conv_w_qkv),
        "b_qkv": np.asarray(L0_conv_b_qkv).reshape(3, C).T,
        "w_proj": np.asarray(L0_conv_w_proj),
        "b_proj": np.asarray(L0_conv_b_proj).reshape(1, C),
        "rel_flipped": np.asarray(L0_conv_rel_table).reshape(span, span, HEADS)[::-1, ::-1]
        .transpose(2, 0, 1).reshape(1, HEADS, span, span),
        "g2": np.asarray(L0_conv_g2).reshape(C, 1),
        "b2": np.asarray(L0_conv_b2).reshape(C, 1),
        "w_fc1": np.asarray(L0_conv_w_fc1),
        "b_fc1": np.asarray(L0_conv_b_fc1).reshape(CHUNKS, C).T,
        "w_fc2": np.asarray(L0_conv_w_fc2),
        "b_fc2": np.asarray(L0_conv_b_fc2).reshape(1, C),
        "mask": window_mask(),
    }
    nc = bacc.Bacc("TRN2", target_bir_lowering=False, num_devices=1)
    arrays, aps = {}, []
    for name, a in laid.items():
        arrays[f"in_{name}"] = np.ascontiguousarray(a)
        aps.append(nc.dram_tensor(f"in_{name}", a.shape, F32, kind="ExternalInput").ap())
    aps.append(nc.dram_tensor("out", (shape[0], IMG, C), F32, kind="ExternalOutput").ap())
    swin_block(nc, *aps)
    r = run_bass_kernel_spmd(nc, [arrays], core_ids=[0])
    return r.results[0]["out"].reshape(shape)
```

```python
from contextlib import ExitStack

import numpy as np

import concourse.bass as bass
from concourse import mybir

F32 = mybir.dt.float32
ALU = mybir.AluOpType
ACT = mybir.ActivationFunctionType
AX_X = mybir.AxisListType.X

ROWS = COLS = 56
C = 128
HEADS = 4
HD = C // HEADS
WIN = 7
SHIFT = 3
N = WIN * WIN
HIDDEN = 4 * C
CHUNKS = HIDDEN // C
WINDOWS = COLS // WIN
PAIRS = WINDOWS // 2
HALF = 64
BANDS = 2
BAND = WINDOWS * N
STEP_ROWS = BANDS * WIN
STEPS = ROWS // STEP_ROWS
TOK = BANDS * COLS
TILES = WIN
STEP = TILES * TOK
IMG = ROWS * COLS
WHOLE = WINDOWS - 1
HEAD = WIN - SHIFT
FIRST = 4
HALVES = ((0, FIRST), (FIRST, TILES))
LOADS = [2, 2, 2, 3]
SCALE = float(HD) ** -0.5
EPS = 1e-5

PER_QKVO = 8
O_USE = (0, 1)
Q_USE, K_USE, V_USE = (2, 4), (3, 5), (6, 7)
BEFORE_STEP_0 = 6


class At:

    def __init__(self, img, s, attn=True, nxt=True, hidden=True, mlp_out=True):
        self.img, self.s = img, s
        self.attn, self.nxt, self.hidden, self.mlp_out = attn, nxt, hidden, mlp_out

    def count(self, per, k, d=0):
        return self.img * (STEPS * per) + ((self.s + d) * per + k)

    def slot(self, d=0):
        return (self.s + d) % STEPS

    def image(self, d=0):
        return self.img + (self.s + d) // STEPS


def wait(eng, sem, value):
    if isinstance(value, int) and value <= 0:
        return
    eng.wait_ge(sem, value)


def run_steps(eng, images, step):
    step(At(-1, STEPS - 1, attn=False, hidden=False, mlp_out=False))
    for s in range(STEPS):
        step(At(0, s, hidden=s > 0, mlp_out=s > 1))
    if images > 2:
        with eng.Fori(1, images - 1) as img:
            for s in range(STEPS):
                step(At(img, s))
    for s in range(STEPS):
        step(At(images - 1, s, nxt=s < STEPS - 1))
    step(At(images, 0, attn=False, nxt=False))
    step(At(images, 1, attn=False, nxt=False, hidden=False))


def swin_block(nc, x, g1, b1, w_qkv, b_qkv, w_proj, b_proj, rel_flipped, g2, b2, w_fc1, b_fc1, w_fc2,
               b_fc2, mask, out):
    images = x.shape[0]

    with ExitStack() as ctx:
        def sb(name, shape, dt=F32):
            return ctx.enter_context(nc.sbuf_tensor(name, shape, dt))

        def sem(name):
            return ctx.enter_context(nc.semaphore(name))

        x_in = sb("x_in", [TOK, STEPS, TILES, C])
        stream = sb("stream", [TOK, STEPS, TILES, C])
        xn1 = sb("xn1", [TOK, TILES, C])
        xn2 = sb("xn2", [TOK, TILES, C])
        raw1 = sb("raw1", [TOK, TILES, 6])
        raw2 = sb("raw2", [TOK, TILES, 6])
        part1 = sb("part1", [TOK, 4, TILES])
        part2 = sb("part2", [TOK, 4, TILES])
        mean1 = sb("mean1", [TOK, TILES])
        mean2 = sb("mean2", [TOK, TILES])
        ve1 = sb("ve1", [TOK, TILES])
        ve2 = sb("ve2", [TOK, TILES])
        rstd1 = sb("rstd1", [TOK, TILES])
        rstd2 = sb("rstd2", [TOK, TILES])
        xT = sb("xT", [C, BANDS, WINDOWS, N])
        qT = sb("qT", [C, BANDS, BAND])
        kT = sb("kT", [C, BANDS, BAND])
        oT = sb("oT", [C, TILES, BANDS, COLS])
        x2T = sb("x2T", [C, STEP])
        hT = sb("hT", [C, CHUNKS, STEP])
        kd = sb("kd", [C, BANDS, HEADS, BAND])
        scores = sb("scores", [128, BANDS, PAIRS, HEADS, N])
        row_max = sb("row_max", [128, BANDS, PAIRS, HEADS])
        row_sum = sb("row_sum", [128, BANDS, PAIRS, HEADS])
        row_inv = sb("row_inv", [128, BANDS, PAIRS, HEADS])
        probs = sb("probs", [128, BANDS, PAIRS, HEADS, HALF])
        probsT = sb("probsT", [128, BANDS, PAIRS, 2, 128])
        vd = sb("vd", [128, BANDS, WINDOWS, 2, 2, HD])
        wqkv = sb("wqkv", [C, 3 * C])
        wq = sb("wq", [C, C])
        wk = sb("wk", [C, C])
        wv = sb("wv", [C, 2, 2, HD])
        wproj = sb("wproj", [C, C])
        wfc1_raw = sb("wfc1_raw", [C, HIDDEN])
        wfc1 = sb("wfc1", [C, HIDDEN])
        wfc2 = sb("wfc2", [C, CHUNKS, C])
        vecs = sb("vecs", [C, 4])
        bqkv = sb("bqkv", [C, 3])
        bfc1 = sb("bfc1", [C, CHUNKS])
        bias_q = sb("bias_q", [C, 1])
        bias_k = sb("bias_k", [C, 1])
        bias_v = sb("bias_v", [C, 1])
        bias_v_wide = sb("bias_v_wide", [C, TOK])
        bias_h = sb("bias_h", [C, CHUNKS])
        brow_proj_in = sb("brow_proj_in", [TOK, C])
        brow_proj = sb("brow_proj", [TOK, C])
        brow_fc2 = sb("brow_fc2", [TOK, C])
        rel = sb("rel", [128, HEADS, N])
        mask_sb = sb("mask_sb", [128, 2, PAIRS, N])
        bias_rel = sb("bias_rel", [128, 2, PAIRS, HEADS, N])
        minus_half = sb("minus_half", [TOK, TILES])
        ident = sb("ident", [128, 128])

        psum = ctx.enter_context(nc.psum_tensor("psum", [128, 8, 512], F32))
        S_BANK, QKVO_BANK, TOK_BANK = 0, 4, 6

        weights_loaded = sem("weights_loaded")
        rel_cleared = sem("rel_cleared")
        rel_loaded = sem("rel_loaded")
        ident_zeroed = sem("ident_zeroed")
        ident_ready = sem("ident_ready")
        weights_ready = sem("weights_ready")
        bias_products = sem("bias_products")
        bias_v_ready = sem("bias_v_ready")
        brow_product = sem("brow_product")
        consts_ready = sem("consts_ready")
        kd_filled = [sem(f"kd_filled{i}") for i in range(BANDS)]
        x_loaded = [sem(f"x_loaded{i}") for i in range(STEPS)]
        out_stored = [sem(f"out_stored{i}") for i in range(STEPS)]
        raw1_done = sem("raw1_done")
        parts1_done = sem("parts1_done")
        stats1_done = sem("stats1_done")
        var1_ready = sem("var1_ready")
        xn1_ready = sem("xn1_ready")
        scores_biased = sem("scores_biased")
        max_done = sem("max_done")
        scores_shifted = sem("scores_shifted")
        sum_done = sem("sum_done")
        inv_ready = sem("inv_ready")
        residual_added = sem("residual_added")
        raw2_done = sem("raw2_done")
        parts2_done = sem("parts2_done")
        stats2_done = sem("stats2_done")
        var2_ready = sem("var2_ready")
        xn2_ready = sem("xn2_ready")
        out_added = sem("out_added")
        x_biased = sem("x_biased")
        rstd1_ready = sem("rstd1_ready")
        probs_normed = sem("probs_normed")
        rstd2_ready = sem("rstd2_ready")
        x1_biased = sem("x1_biased")
        xT_made = sem("xT_made")
        qkvo_made = sem("qkvo_made")
        scores_made = sem("scores_made")
        probsT_made = sem("probsT_made")
        proj_made = sem("proj_made")
        x2T_made = sem("x2T_made")
        fc1_made = sem("fc1_made")
        fc2_made = sem("fc2_made")
        xT_copied = sem("xT_copied")
        qkvo_copied = sem("qkvo_copied")
        exp_done = sem("exp_done")
        probsT_copied = sem("probsT_copied")
        x2T_copied = sem("x2T_copied")
        gelu_done = sem("gelu_done")

        def qkvo_psum(use):
            return psum[:, QKVO_BANK + use % 2, :]

        def scores_psum(band):
            b = psum[:, S_BANK + 2 * band:S_BANK + 2 * band + 2, 0:2 * HEADS * N]
            return b.rearrange("p b (a n) -> p b a n", a=2)

        def tok_psum(use):
            return psum[:, TOK_BANK + use % 2, :]

        def qkvo_count(at, use, d=0):
            return at.count(PER_QKVO, BEFORE_STEP_0 + use + 1, d)

        FC2, X2T, FC1, XT, PROJ = 0, 2, 4, 12, 14

        def token_pieces(s, dram, img, tile):
            pieces = []
            for band in range(BANDS):
                row = STEP_ROWS * s + WIN * band + SHIFT
                whole = min(WIN, ROWS - row)
                for first, t0, t1 in ((row, 0, whole), (0, whole, WIN)):
                    if t0 < t1:
                        rows = dram[img, first * COLS:(first + t1 - t0) * COLS, :]
                        pieces.append((rows.rearrange("(t p) c -> p t c", p=COLS),
                                       tile[COLS * band:COLS * (band + 1), t0:t1, :]))
            assert len(pieces) == LOADS[s]
            return pieces

        def dma_count(s, img):
            return img * (16 * LOADS[s]) + 16 * LOADS[s]

        def load_rel(eng, half):
            eng.wait_ge(rel_cleared, 1)
            for ni in range(WIN):
                for nj in range(WIN):
                    p = HALF * half + WIN * ni + nj
                    i0, j0 = WIN - 1 - ni, WIN - 1 - nj
                    eng.dma_start(rel[p:p + 1, :, :].rearrange("p h (i j) -> p h i j", i=WIN),
                                  rel_flipped[:, :, i0:i0 + WIN, j0:j0 + WIN]).then_inc(rel_loaded, 16)

        block = ctx.enter_context(nc.Block())

        @block.sync
        def _(sp):
            def load(img, s):
                for src, dst in token_pieces(s, x, img, x_in[:, s, :, :]):
                    sp.dma_start(dst, src).then_inc(x_loaded[s], 16)

            def store(img, s):
                for dst, src in token_pieces(s, out, img, stream[:, s, :, :]):
                    sp.dma_start(dst, src).then_inc(out_stored[s], 16)

            load(0, 0)
            for dst, src in ((wqkv[:, :], w_qkv), (vecs[:, 0:1], g1), (vecs[:, 1:2], b1), (vecs[:, 2:3], g2),
                             (vecs[:, 3:4], b2), (bqkv[:, :], b_qkv), (wproj[:, :], w_proj),
                             (wfc1_raw[:, :], w_fc1), (bfc1[:, :], b_fc1),
                             (wfc2[:, :, :], w_fc2.rearrange("(k p) n -> p k n", p=C)),
                             (brow_proj_in[:, :], b_proj.to_broadcast([TOK, C])),
                             (brow_fc2[:, :], b_fc2.to_broadcast([TOK, C])),
                             (mask_sb[:, :, :, :], mask)):
                sp.dma_start(dst, src).then_inc(weights_loaded, 16)
            load_rel(sp, 0)
            for s in range(1, STEPS):
                load(0, s)

            def fill_kd(at, band):
                wait(sp, qkvo_copied, qkvo_count(at, K_USE[band]))
                for h in range(HEADS):
                    rows = slice(HD * h, HD * (h + 1))
                    sp.dma_start(kd[rows, band, h, :], kT[rows, band, :]).then_inc(kd_filled[band], 16)

            def step(at):
                if at.mlp_out:
                    wait(sp, out_added, at.count(2, 2, -2))
                    store(at.image(-2), at.slot(-2))
                if at.nxt:
                    fill_kd(at, 0)
                    fill_kd(at, 1)
                if at.attn and not (isinstance(at.img, int) and at.img == images - 1):
                    wait(sp, residual_added, at.count(2, 1))
                    load(at.image(STEPS), at.slot())

            run_steps(sp, images, step)
            for s in range(STEPS):
                sp.wait_ge(out_stored[s], dma_count(s, images - 1))

        @block.gpsimd
        def _(pool):
            pool.memset(ident[:, :], 0.0).then_inc(ident_zeroed, 1)
            pool.wait_ge(ident_zeroed, 1)
            pool.affine_select(out=ident[:, :], in_=ident[:, :], compare_op=ALU.not_equal, fill=1.0, base=0,
                               pattern=[[-1, 128]], channel_multiplier=1).then_inc(ident_ready, 1)
            pool.memset(minus_half[:, :], -0.5).then_inc(consts_ready, 1)
            pool.wait_ge(consts_ready, 2)
            pool.wait_ge(weights_loaded, 13 * 16)

            def step(at):
                if at.hidden:
                    wait(pool, xn2_ready, at.count(2, 2, -1))
                    pool.tensor_tensor(stream[:, at.slot(-1), :, :], stream[:, at.slot(-1), :, :],
                                       brow_fc2[:, :].unsqueeze(1).to_broadcast([TOK, TILES, C]),
                                       ALU.add).then_inc(x1_biased, 1)
                if at.attn:
                    for band in range(BANDS):
                        wait(pool, inv_ready, at.count(2, band + 1))
                        p = probs[:, band, :, :, 0:N].rearrange("p a h m -> p (a h) m")
                        r = row_inv[:, band, :, :].rearrange("p a h -> p (a h)")
                        pool.tensor_tensor(p, p, r.unsqueeze(2).to_broadcast([128, PAIRS * HEADS, N]),
                                           ALU.mult).then_inc(probs_normed, 1)
                if at.nxt:
                    wait(pool, var1_ready, at.count(1, 1, 1))
                    pool.tensor_tensor(rstd1[:, :], ve1[:, :], minus_half[:, :], ALU.pow).then_inc(rstd1_ready, 1)
                    wait(pool, x_loaded[at.slot(1)], dma_count(at.slot(1), at.image(1)))
                    before = at.image(1) - 1
                    wait(pool, out_stored[at.slot(1)],
                         0 if isinstance(before, int) and before < 0 else dma_count(at.slot(1), before))
                    pool.tensor_tensor(stream[:, at.slot(1), :, :], x_in[:, at.slot(1), :, :],
                                       brow_proj[:, :].unsqueeze(1).to_broadcast([TOK, TILES, C]),
                                       ALU.add).then_inc(x_biased, 1)
                if at.attn:
                    wait(pool, var2_ready, at.count(1, 1))
                    pool.tensor_tensor(rstd2[:, :], ve2[:, :], minus_half[:, :], ALU.pow).then_inc(rstd2_ready, 1)

            run_steps(pool, images, step)

        @block.scalar
        def _(act):
            load_rel(act, 1)
            act.wait_ge(weights_ready, 1)
            act.wait_ge(consts_ready, 2)

            def columns_shifted(image, windows, copy):
                last = windows[:, WHOLE, :, :]
                copy(image[:, :, SHIFT:SHIFT + WHOLE * WIN].rearrange("c i (w j) -> c w i j", j=WIN),
                     windows[:, 0:WHOLE, :, :])
                copy(image[:, :, COLS - HEAD:COLS], last[:, :, 0:HEAD])
                return copy(image[:, :, 0:SHIFT], last[:, :, HEAD:WIN])

            def exp(at, band):
                wait(act, scores_shifted, at.count(2, band + 1))
                wait(act, probsT_made, at.count(4, 2 * band + 2, -1))
                act.activation(probs[:, band, :, :, 0:N].rearrange("p a h m -> p (a h) m"),
                               scores[:, band, :, :, :].rearrange("p a h m -> p (a h) m"), ACT.Exp).then_inc(exp_done, 1)

            def copy_probsT(at, band):
                for f in range(2):
                    wait(act, probsT_made, at.count(4, 2 * band + f + 1))
                    act.activation(probsT[:, band, 2 * f:2 * f + 2, :, :].rearrange("p a q n -> p (a q n)"),
                                   psum[:, S_BANK + 2 * band + f, :], ACT.Copy).then_inc(probsT_copied, 1)

            def copy_o(at, band):
                use = O_USE[band]
                wait(act, qkvo_made, qkvo_count(at, use))
                windows = qkvo_psum(use)[:, 0:BAND].rearrange("c (w i j) -> c w i j", i=WIN, j=WIN)
                columns_shifted(oT[:, :, band, :], windows,
                                lambda image, win: act.activation(image, win, ACT.Copy)).then_inc(qkvo_copied, 1)

            def copy_x(h):
                t0, t1 = HALVES[h]
                for band in range(BANDS):
                    rows = tok_psum(XT + h)[:, 0:(t1 - t0) * TOK].rearrange("c (t b j) -> c t b j", b=BANDS, j=COLS)
                    windows = xT[:, band, :, :].rearrange("c w (i j) -> c w i j", j=WIN)
                    last = columns_shifted(rows[:, :, band, :], windows[:, :, t0:t1, :],
                                           lambda image, win: act.activation(win, image, ACT.Copy))
                return last

            def copy_qk(at, band):
                wait(act, kd_filled[band], at.count(16 * HEADS, 16 * HEADS))
                for use, dst, bias in ((Q_USE[band], qT, bias_q), (K_USE[band], kT, bias_k)):
                    wait(act, qkvo_made, qkvo_count(at, use))
                    act.activation(dst[:, band, :], qkvo_psum(use)[:, 0:BAND], ACT.Identity,
                                   bias=bias[:, :]).then_inc(qkvo_copied, 1)

            def copy_v(at, band):
                use = V_USE[band]
                wait(act, qkvo_made, qkvo_count(at, use))
                for hp in range(2):
                    p = slice(HALF * hp, HALF * hp + N)
                    v = qkvo_psum(use)[p, :].rearrange("m (w q d) -> m w q d", w=WINDOWS, q=2)
                    last = act.activation(vd[p, band, :, :, hp, :], v, ACT.Copy)
                last.then_inc(qkvo_copied, 1)

            def gelu(at, n):
                band, chunk = divmod(n, CHUNKS)
                wait(act, fc1_made, at.count(BANDS * CHUNKS, n + 1, -1))
                act.activation(hT[:, chunk, band * BAND:(band + 1) * BAND], tok_psum(FC1 + n)[:, 0:BAND],
                               ACT.Gelu, bias=bias_h[:, chunk:chunk + 1]).then_inc(gelu_done, 1)

            def step(at):
                if at.attn:
                    exp(at, 0)
                    exp(at, 1)
                if at.hidden:
                    for h, (t0, t1) in enumerate(HALVES):
                        wait(act, x2T_made, at.count(2, h + 1, -1))
                        act.activation(x2T[:, t0 * TOK:t1 * TOK], tok_psum(X2T + h)[:, 0:(t1 - t0) * TOK],
                                       ACT.Copy).then_inc(x2T_copied, 1)
                for band in range(BANDS):
                    if at.hidden:
                        gelu(at, 4 * band)
                        gelu(at, 4 * band + 1)
                    if at.attn:
                        copy_probsT(at, band)
                    if at.hidden:
                        gelu(at, 4 * band + 2)
                        gelu(at, 4 * band + 3)
                    if at.attn and band == 0:
                        copy_o(at, 0)
                if at.nxt:
                    for h in range(2):
                        wait(act, xT_made, at.count(2, h + 1, 1))
                        copy_x(h).then_inc(xT_copied, 1)
                if at.attn:
                    copy_o(at, 1)
                if at.nxt:
                    copy_qk(at, 0)
                    copy_qk(at, 1)
                    copy_v(at, 0)
                    copy_v(at, 1)

            run_steps(act, images, step)

        @block.vector
        def _(dve):
            dve.memset(rel[:, :, :], 0.0).then_inc(rel_cleared, 1)
            dve.memset(probs[:, :, :, :, :], 0.0)
            dve.memset(kd[:, :, :, :], 0.0)
            dve.memset(vd[:, :, :, :, :, :], 0.0)
            dve.memset(psum[:, 0:4, :], 0.0).then_inc(weights_ready, 1)
            dve.wait_ge(weights_loaded, 13 * 16)
            dve.tensor_scalar(wq[:, :], wqkv[:, 0:C], vecs[:, 0:1], SCALE, ALU.mult, ALU.mult)
            dve.tensor_scalar(wk[:, :], wqkv[:, C:2 * C], vecs[:, 0:1], None, ALU.mult)
            dve.tensor_scalar(wv[:, :, :, :].rearrange("c p q d -> c q p d"),
                              wqkv[:, 2 * C:3 * C].rearrange("c (q p d) -> c q p d", q=2, p=2),
                              vecs[:, 0:1], None, ALU.mult)
            dve.tensor_scalar(wfc1[:, :], wfc1_raw[:, :], vecs[:, 2:3], None, ALU.mult).then_inc(weights_ready, 1)
            dve.wait_ge(bias_products, 1)
            made = psum[:, QKVO_BANK, :]
            dve.tensor_scalar(bias_q[:, :], made[:, 0:1], bqkv[:, 0:1], SCALE, ALU.add, ALU.mult)
            dve.tensor_tensor(bias_k[:, :], made[:, 1:2], bqkv[:, 1:2], ALU.add)
            dve.tensor_tensor(bias_v[:, :], made[:, 2:3], bqkv[:, 2:3], ALU.add)
            dve.tensor_tensor(bias_h[:, :], made[:, 3:3 + CHUNKS], bfc1[:, :], ALU.add).then_inc(bias_v_ready, 1)
            dve.wait_ge(bias_v_ready, 1)
            dve.tensor_copy(bias_v_wide[:, :], bias_v[:, 0:1].to_broadcast([C, TOK])).then_inc(bias_v_ready, 1)
            dve.wait_ge(brow_product, 1)
            dve.tensor_tensor(brow_proj[:, :], psum[0:TOK, QKVO_BANK + 1, 0:C], brow_proj_in[:, :], ALU.add)
            dve.wait_ge(rel_loaded, 2 * N * 16)
            for last_band in range(2):
                for h in range(HEADS):
                    last = dve.tensor_tensor(bias_rel[:, last_band, :, h, :], mask_sb[:, last_band, :, :],
                                             rel[:, h, :].unsqueeze(1).to_broadcast([128, PAIRS, N]), ALU.add)
            last.then_inc(consts_ready, 1)
            dve.wait_ge(consts_ready, 2)

            def raw_stats(src, raw, t0, t1):
                for t in range(t0, t1):
                    last = dve.bn_stats(raw[:, t, :], src[:, t, :])
                return last

            def mean_var(raw, part, mean, ve, raw_done, parts_done, stats_done, ready, n):
                mean0, mean1 = raw[:, :, 1], raw[:, :, 4]
                wait(dve, raw_done, n)
                dve.tensor_tensor(part[:, 0, :], mean0, mean1, ALU.add)
                dve.tensor_tensor(part[:, 1, :], mean0, mean1, ALU.subtract)
                dve.scalar_tensor_tensor(part[:, 2, :], raw[:, :, 2], C * EPS, raw[:, :, 5], ALU.add,
                                         ALU.add).then_inc(parts_done, 1)
                wait(dve, parts_done, n)
                dve.tensor_scalar(mean[:, :], part[:, 0, :], 0.5, None, ALU.mult)
                dve.scalar_tensor_tensor(part[:, 3, :], part[:, 1, :], 0.25, part[:, 1, :], ALU.mult,
                                         ALU.mult).then_inc(stats_done, 1)
                wait(dve, stats_done, n)
                dve.scalar_tensor_tensor(ve[:, :], part[:, 2, :], 1.0 / C, part[:, 3, :], ALU.mult,
                                         ALU.add).then_inc(ready, 1)

            def normalise(dst, src, mean, rstd, ready):
                for t0, t1 in HALVES:
                    for t in range(t0, t1):
                        last = dve.tensor_scalar(dst[:, t, :], src[:, t, :], mean[:, t:t + 1], rstd[:, t:t + 1],
                                                 ALU.subtract, ALU.mult)
                    last.then_inc(ready, 1)

            def shift_scores(at, band):
                sc = scores[:, band, :, :, :].rearrange("p (b a) h m -> p b (a h m)", b=2)
                rows = scores[:, band, :, :, :].rearrange("p a h m -> p (a h) m")
                mx = row_max[:, band, :, :].rearrange("p a h -> p (a h)")
                last_band = int(at.s == STEPS - 1 and band == BANDS - 1)
                wait(dve, scores_made, at.count(2, band + 1))
                wait(dve, exp_done, at.count(2, band + 1, -1))
                dve.tensor_tensor(sc, scores_psum(band).rearrange("p b a n -> p b (a n)"),
                                  bias_rel[:, last_band, :, :, :].rearrange("p (b a) h m -> p b (a h m)", b=2),
                                  ALU.add).then_inc(scores_biased, 1)
                wait(dve, scores_biased, at.count(2, band + 1))
                dve.tensor_reduce(mx, rows, AX_X, ALU.max).then_inc(max_done, 1)
                wait(dve, max_done, at.count(2, band + 1))
                dve.tensor_tensor(rows, rows, mx.unsqueeze(2).to_broadcast([128, HEADS * PAIRS, N]),
                                  ALU.subtract).then_inc(scores_shifted, 1)

            def inverse_sums(at, band):
                p = probs[:, band, :, :, 0:N].rearrange("p a h m -> p (a h) m")
                s = row_sum[:, band, :, :].rearrange("p a h -> p (a h)")
                r = row_inv[:, band, :, :].rearrange("p a h -> p (a h)")
                wait(dve, exp_done, at.count(2, band + 1))
                dve.tensor_reduce(s, p, AX_X, ALU.add).then_inc(sum_done, 1)
                wait(dve, sum_done, at.count(2, band + 1))
                dve.reciprocal(r, s).then_inc(inv_ready, 1)

            def add_to_stream(slot, use, h):
                t0, t1 = HALVES[h]
                s = stream[:, slot, t0:t1, :].rearrange("p t c -> p (t c)")
                return dve.tensor_tensor(s, tok_psum(use)[0:TOK, 0:(t1 - t0) * C], s, ALU.add)

            def add_mlp(at, h):
                wait(dve, x1_biased, at.count(1, 1, -2))
                wait(dve, fc2_made, at.count(2, h + 1, -2))
                add_to_stream(at.slot(-2), FC2 + h, h).then_inc(out_added, 1)

            def step(at):
                if at.attn:
                    shift_scores(at, 0)
                if at.hidden:
                    wait(dve, rstd2_ready, at.count(1, 1, -1))
                    wait(dve, x2T_made, at.count(2, 2, -2))
                    normalise(xn2, stream[:, at.slot(-1), :, :], mean2, rstd2, xn2_ready)
                if at.mlp_out:
                    add_mlp(at, 0)
                if at.attn:
                    shift_scores(at, 1)
                if at.mlp_out:
                    add_mlp(at, 1)
                if at.attn:
                    inverse_sums(at, 0)
                    inverse_sums(at, 1)
                if at.nxt:
                    wait(dve, x_loaded[at.slot(1)], dma_count(at.slot(1), at.image(1)))
                    wait(dve, xn1_ready, at.count(2, 2))
                    raw_stats(x_in[:, at.slot(1), :, :], raw1, 0, TILES).then_inc(raw1_done, 1)
                    mean_var(raw1, part1, mean1, ve1, raw1_done, parts1_done, stats1_done, var1_ready,
                             at.count(1, 1, 1))
                    wait(dve, rstd1_ready, at.count(1, 1, 1))
                    wait(dve, xT_made, at.count(2, 2))
                    normalise(xn1, x_in[:, at.slot(1), :, :], mean1, rstd1, xn1_ready)
                if at.attn:
                    wait(dve, x_biased, at.count(1, 1))
                    for h in range(2):
                        wait(dve, proj_made, at.count(2, h + 1))
                        add_to_stream(at.slot(), PROJ + h, h).then_inc(residual_added, 1)
                    wait(dve, xn2_ready, at.count(2, 2, -1))
                    for h, (t0, t1) in enumerate(HALVES):
                        wait(dve, residual_added, at.count(2, h + 1))
                        last = raw_stats(stream[:, at.slot(), :, :], raw2, t0, t1)
                    last.then_inc(raw2_done, 1)
                    mean_var(raw2, part2, mean2, ve2, raw2_done, parts2_done, stats2_done, var2_ready, at.count(1, 1))

            run_steps(dve, images, step)

        @block.tensor
        def _(pe):
            pe.wait_ge(weights_loaded, 13 * 16)
            for k in range(3):
                pe.matmul(psum[:, QKVO_BANK, k:k + 1], wqkv[:, k * C:(k + 1) * C], vecs[:, 1:2],
                          start=True, stop=True)
            for k in range(CHUNKS):
                last = pe.matmul(psum[:, QKVO_BANK, 3 + k:4 + k], wfc1_raw[:, k * C:(k + 1) * C], vecs[:, 3:4],
                                 start=True, stop=True)
            last.then_inc(bias_products, 1)
            pe.wait_ge(bias_v_ready, 2)
            pe.matmul(psum[0:TOK, QKVO_BANK + 1, 0:C], bias_v_wide[:, :], wproj[:, :], start=True,
                      stop=True).then_inc(brow_product, 1)
            pe.wait_ge(weights_ready, 2)
            pe.wait_ge(ident_ready, 1)
            pe.wait_ge(consts_ready, 2)

            def make_scores(band):
                for w in range(WINDOWS):
                    half, pair = HALF * (w % 2), w // 2
                    cols = slice(w * N, (w + 1) * N)
                    last = pe.matmul(scores_psum(band)[half:half + N, pair // 2, pair % 2, :],
                                     qT[:, band, cols], kd[:, band, :, cols], start=True, stop=True)
                last.then_inc(scores_made, 1)

            def transpose_tiles(src, use, h):
                t0, t1 = HALVES[h]
                for t in range(t0, t1):
                    last = pe.transpose(tok_psum(use)[:, (t - t0) * TOK:(t - t0 + 1) * TOK], src[:, t, :],
                                        ident[0:TOK, 0:TOK])
                return last

            def transpose_probs(at, band):
                wait(pe, probs_normed, at.count(2, band + 1))
                for f in range(2):
                    for n in range(4):
                        pair, hq = 2 * f + n // 2, n % 2
                        last = pe.transpose(psum[:, S_BANK + 2 * band + f, 128 * n:128 * (n + 1)],
                                            probs[:, band, pair, 2 * hq:2 * hq + 2, :].rearrange("p h m -> p (h m)"),
                                            ident[:, :])
                    last.then_inc(probsT_made, 1)

            def attend(at, band):
                wait(pe, probsT_copied, at.count(4, 2 * band + 2))
                wait(pe, qkvo_copied, qkvo_count(at, V_USE[band], -1))
                for w in range(WINDOWS):
                    for hq in range(2):
                        last = pe.matmul(qkvo_psum(O_USE[band])[HALF * hq:HALF * (hq + 1), w * N:(w + 1) * N],
                                         vd[:, band, w, hq, :, :].rearrange("m p d -> m (p d)"),
                                         probsT[:, band, w // 2, hq, HALF * (w % 2):HALF * (w % 2) + N],
                                         start=True, stop=True)
                last.then_inc(qkvo_made, 1)

            def make_qk(at, band):
                wait(pe, xT_copied, at.count(2, 2, 1))
                for use, w in ((Q_USE[band], wq), (K_USE[band], wk)):
                    wait(pe, qkvo_copied, qkvo_count(at, use - 2))
                    pe.matmul(qkvo_psum(use)[:, 0:BAND], w[:, :], xT[:, band, :, :].rearrange("c w n -> c (w n)"),
                              start=True, stop=True).then_inc(qkvo_made, 1)

            def make_values(band):
                use = V_USE[band]
                for w in range(WINDOWS):
                    for hp in range(2):
                        last = pe.matmul(qkvo_psum(use)[HALF * hp:HALF * hp + N, w * HALF:(w + 1) * HALF],
                                         xT[:, band, w, :], wv[:, hp, :, :].rearrange("c q d -> c (q d)"),
                                         start=True, stop=True)
                last.then_inc(qkvo_made, 1)

            def project(at, h):
                t0, t1 = HALVES[h]
                for t in range(t0, t1):
                    last = pe.matmul(tok_psum(PROJ + h)[0:TOK, (t - t0) * C:(t - t0 + 1) * C],
                                     oT[:, t, :, :].rearrange("c b j -> c (b j)"), wproj[:, :], start=True, stop=True)
                last.then_inc(proj_made, 1)

            def make_hidden(at, n):
                band, chunk = divmod(n, CHUNKS)
                if n < 2:
                    wait(pe, x2T_copied, at.count(2, n + 1, -1))
                else:
                    wait(pe, gelu_done, at.count(BANDS * CHUNKS, n - 1, -1))
                pe.matmul(tok_psum(FC1 + n)[:, 0:BAND], wfc1[:, chunk * C:(chunk + 1) * C],
                          x2T[:, band * BAND:(band + 1) * BAND], start=True, stop=True).then_inc(fc1_made, 1)

            def make_out(at, h):
                if at.hidden:
                    wait(pe, residual_added, at.count(2, h + 1, -1))
                t0, t1 = HALVES[h]
                for t in range(t0, t1):
                    for chunk in range(CHUNKS):
                        last = pe.matmul(tok_psum(FC2 + h)[0:TOK, (t - t0) * C:(t - t0 + 1) * C],
                                         hT[:, chunk, t * TOK:(t + 1) * TOK], wfc2[:, chunk, :],
                                         start=chunk == 0, stop=chunk == CHUNKS - 1)
                last.then_inc(fc2_made, 1)

            def step(at):
                for band in range(BANDS):
                    if at.attn:
                        wait(pe, kd_filled[band], at.count(16 * HEADS, 16 * HEADS))
                        wait(pe, probsT_copied, at.count(4, 2 * band + 2, -1))
                        make_scores(band)
                    if at.mlp_out:
                        wait(pe, gelu_done, at.count(BANDS * CHUNKS, BANDS * CHUNKS, -2))
                        make_out(at, band)
                if at.hidden:
                    for h in range(2):
                        wait(pe, xn2_ready, at.count(2, h + 1, -1))
                        wait(pe, out_added, at.count(2, h + 1, -2))
                        transpose_tiles(xn2, X2T + h, h).then_inc(x2T_made, 1)
                for band in range(BANDS):
                    if at.hidden:
                        make_hidden(at, 4 * band)
                        make_hidden(at, 4 * band + 1)
                    if at.attn:
                        transpose_probs(at, band)
                    if at.hidden:
                        make_hidden(at, 4 * band + 2)
                        make_hidden(at, 4 * band + 3)
                    if at.attn and band == 0:
                        attend(at, 0)
                if at.nxt:
                    for h in range(2):
                        wait(pe, xn1_ready, at.count(2, h + 1, 1))
                        wait(pe, gelu_done, at.count(BANDS * CHUNKS, BANDS * CHUNKS - 1 + h, -1))
                        transpose_tiles(xn1, XT + h, h).then_inc(xT_made, 1)
                if at.attn:
                    attend(at, 1)
                if at.nxt:
                    make_qk(at, 0)
                    make_qk(at, 1)
                if at.attn:
                    wait(pe, qkvo_copied, qkvo_count(at, O_USE[1]))
                    for h in range(2):
                        if at.nxt:
                            wait(pe, xT_copied, at.count(2, h + 1, 1))
                        else:
                            wait(pe, gelu_done, at.count(BANDS * CHUNKS, BANDS * CHUNKS - 1 + h, -1))
                        project(at, h)
                if at.nxt:
                    for band in range(BANDS):
                        wait(pe, qkvo_copied, qkvo_count(at, V_USE[band] - 2))
                        make_values(band)

            run_steps(pe, images, step)


def window_mask():
    part = np.zeros((2, WIN), np.int64)
    part[1, WIN - SHIFT:] = 1
    full = np.zeros((128, 2, PAIRS, N), np.float32)
    for last_band in range(2):
        for w in range(WINDOWS):
            region = (2 * part[last_band][:, None] + part[int(w == WINDOWS - 1)][None, :]).reshape(-1)
            differ = region[:, None] != region[None, :]
            p0 = HALF * (w % 2)
            full[p0:p0 + N, last_band, w // 2, :] = np.where(differ, -100.0, 0.0)
    return full


def kernel(x, L0_conv_g1, L0_conv_b1, L0_conv_w_qkv, L0_conv_b_qkv, L0_conv_w_proj, L0_conv_b_proj,
           L0_conv_rel_table, L0_conv_g2, L0_conv_b2, L0_conv_w_fc1, L0_conv_b_fc1, L0_conv_w_fc2,
           L0_conv_b_fc2):
    import concourse.bacc as bacc
    from concourse.bass_utils import run_bass_kernel_spmd

    x = np.asarray(x)
    shape = x.shape
    span = 2 * WIN - 1
    laid = {
        "x": x.reshape(shape[0], IMG, C),
        "g1": np.asarray(L0_conv_g1).reshape(C, 1),
        "b1": np.asarray(L0_conv_b1).reshape(C, 1),
        "w_qkv": np.asarray(L0_conv_w_qkv),
        "b_qkv": np.asarray(L0_conv_b_qkv).reshape(3, C).T,
        "w_proj": np.asarray(L0_conv_w_proj),
        "b_proj": np.asarray(L0_conv_b_proj).reshape(1, C),
        "rel_flipped": np.asarray(L0_conv_rel_table).reshape(span, span, HEADS)[::-1, ::-1]
        .transpose(2, 0, 1).reshape(1, HEADS, span, span),
        "g2": np.asarray(L0_conv_g2).reshape(C, 1),
        "b2": np.asarray(L0_conv_b2).reshape(C, 1),
        "w_fc1": np.asarray(L0_conv_w_fc1),
        "b_fc1": np.asarray(L0_conv_b_fc1).reshape(CHUNKS, C).T,
        "w_fc2": np.asarray(L0_conv_w_fc2),
        "b_fc2": np.asarray(L0_conv_b_fc2).reshape(1, C),
        "mask": window_mask(),
    }
    nc = bacc.Bacc("TRN2", target_bir_lowering=False, num_devices=1)
    arrays, aps = {}, []
    for name, a in laid.items():
        arrays[f"in_{name}"] = np.ascontiguousarray(a)
        aps.append(nc.dram_tensor(f"in_{name}", a.shape, F32, kind="ExternalInput").ap())
    aps.append(nc.dram_tensor("out", (shape[0], IMG, C), F32, kind="ExternalOutput").ap())
    swin_block(nc, *aps)
    r = run_bass_kernel_spmd(nc, [arrays], core_ids=[0])
    return r.results[0]["out"].reshape(shape)
```

```python
from contextlib import ExitStack

import numpy as np

import concourse.bass as bass
from concourse import mybir

F32 = mybir.dt.float32
F32R = mybir.dt.float32r
ALU = mybir.AluOpType
ACT = mybir.ActivationFunctionType
AX_X = mybir.AxisListType.X

ROWS = COLS = 56
C = 128
HEADS = 4
HD = C // HEADS
WIN = 7
SHIFT = 3
N = WIN * WIN
HIDDEN = 4 * C
CHUNKS = HIDDEN // C
WINDOWS = COLS // WIN
PAIRS = WINDOWS // 2
HALF = 64
BANDS = 2
BAND = WINDOWS * N
STEP_ROWS = BANDS * WIN
STEPS = ROWS // STEP_ROWS
TOK = BANDS * COLS
TILES = WIN
STEP = TILES * TOK
IMG = ROWS * COLS
WHOLE = WINDOWS - 1
HEAD = WIN - SHIFT
FIRST = 4
HALVES = ((0, FIRST), (FIRST, TILES))
LOADS = [2, 2, 2, 3]
SCALE = float(HD) ** -0.5
EPS = 1e-5

class At:

    def __init__(self, images, img, s):
        self.images, self.img, self.s = images, img, s

    def has(self, d=0):
        return not isinstance(self.img, int) or 0 <= self.img * STEPS + self.s + d < self.images * STEPS

    def count(self, per, k, d=0):
        return self.img * (STEPS * per) + ((self.s + d) * per + k)

    def slot(self, d=0):
        return (self.s + d) % STEPS

    def image(self, d=0):
        return self.img + (self.s + d) // STEPS


def wait(eng, sem, value):
    if isinstance(value, int) and value <= 0:
        return
    eng.wait_ge(sem, value)


def run_steps(eng, images, step):
    step(At(images, -1, STEPS - 2))
    step(At(images, -1, STEPS - 1))
    for s in range(STEPS):
        step(At(images, 0, s))
    if images > 2:
        with eng.Fori(1, images - 1) as img:
            for s in range(STEPS):
                step(At(images, img, s))
    for s in range(STEPS):
        step(At(images, images - 1, s))
    step(At(images, images, 0))
    step(At(images, images, 1))


def swin_block(nc, x, g1, b1, w_qkv, b_qkv, w_proj, b_proj, rel_slices, g2, b2, w_fc1, b_fc1, w_fc2,
               b_fc2, mask, out):
    images = x.shape[0]

    with ExitStack() as ctx:
        def sb(name, shape, dt=F32):
            return ctx.enter_context(nc.sbuf_tensor(name, shape, dt))

        def sem(name):
            return ctx.enter_context(nc.semaphore(name))

        x_in = sb("x_in", [TOK, STEPS, TILES, C])
        stream = sb("stream", [TOK, STEPS, TILES, C])
        xn1 = sb("xn1", [TOK, TILES, C])
        xn2 = sb("xn2", [TOK, TILES, C])
        raw1 = sb("raw1", [TOK, TILES, 6])
        raw2 = sb("raw2", [TOK, TILES, 6])
        part1 = sb("part1", [TOK, 4, TILES])
        part2 = sb("part2", [TOK, 4, TILES])
        mean1 = sb("mean1", [TOK, TILES])
        mean2 = sb("mean2", [TOK, TILES])
        ve1 = sb("ve1", [TOK, TILES])
        ve2 = sb("ve2", [TOK, TILES])
        rstd1 = sb("rstd1", [TOK, TILES])
        rstd2 = sb("rstd2", [TOK, TILES])
        xT = sb("xT", [C, 2, BANDS, WINDOWS, HALF])
        xT_hi = sb("xT_hi", [C, BAND], F32R)
        xT_lo = sb("xT_lo", [C, BAND], F32R)
        qT = sb("qT", [C, BANDS, BAND])
        kT = sb("kT", [C, BANDS, BAND])
        oT = sb("oT", [C, TILES, BANDS, COLS])
        x2T_hi = sb("x2T_hi", [C, STEP], F32R)
        x2T_lo = sb("x2T_lo", [C, STEP], F32R)
        hT = sb("hT", [C, CHUNKS, STEP])
        kd = sb("kd", [C, BANDS, HEADS, BAND])
        scores = sb("scores", [128, BANDS, PAIRS, HEADS, N])
        row_max = sb("row_max", [128, BANDS, PAIRS, HEADS])
        row_sum = sb("row_sum", [128, BANDS, PAIRS, HEADS])
        row_inv = sb("row_inv", [128, BANDS, PAIRS, HEADS])
        probs = sb("probs", [128, BANDS, PAIRS, HEADS, HALF])
        probsT = sb("probsT", [128, BANDS, PAIRS, 2, 128])
        vd = sb("vd", [128, BANDS, WINDOWS, 2, 2, HD])
        wqkv = sb("wqkv", [C, 3 * C])
        wqk = sb("wqk", [C, 2, C])
        wqk_hi = sb("wqk_hi", [C, 2, C], F32R)
        wqk_lo = sb("wqk_lo", [C, 2, C], F32R)
        wv = sb("wv", [C, C])
        wproj = sb("wproj", [C, C])
        wfc1_raw = sb("wfc1_raw", [C, HIDDEN])
        wfc1 = sb("wfc1", [C, HIDDEN])
        wfc1_hi = sb("wfc1_hi", [C, HIDDEN], F32R)
        wfc1_lo = sb("wfc1_lo", [C, HIDDEN], F32R)
        wfc2 = sb("wfc2", [C, CHUNKS, C])
        vecs = sb("vecs", [C, 4])
        bqkv = sb("bqkv", [C, 3])
        bfc1 = sb("bfc1", [C, CHUNKS])
        bias_q = sb("bias_q", [C, 1])
        bias_k = sb("bias_k", [C, 1])
        bias_v = sb("bias_v", [C, 1])
        bias_v_wide = sb("bias_v_wide", [C, TOK])
        bias_h = sb("bias_h", [C, CHUNKS])
        brow_proj_in = sb("brow_proj_in", [TOK, C])
        brow_proj = sb("brow_proj", [TOK, C])
        brow_fc2 = sb("brow_fc2", [TOK, C])
        rel = sb("rel", [128, HEADS, N])
        mask_sb = sb("mask_sb", [128, 2, PAIRS, N])
        bias_rel = sb("bias_rel", [128, 2, PAIRS, HEADS, N])
        minus_half = sb("minus_half", [TOK, TILES])
        ident = sb("ident", [128, 128])
        table_probe = sb("table_probe", [C, 1])

        psum = ctx.enter_context(nc.psum_tensor("psum", [128, 8, 512], F32))
        S_BANK, QKVO_BANK, TOK_BANK = 0, 4, 6

        weights_loaded = sem("weights_loaded")
        rel_cleared = sem("rel_cleared")
        rel_loaded = sem("rel_loaded")
        ident_zeroed = sem("ident_zeroed")
        ident_ready = sem("ident_ready")
        weights_ready = sem("weights_ready")
        weights_scaled = sem("weights_scaled")
        bias_products = sem("bias_products")
        bias_v_ready = sem("bias_v_ready")
        brow_product = sem("brow_product")
        minus_half_ready = sem("minus_half_ready")
        brow_ready = sem("brow_ready")
        bias_rel_ready = sem("bias_rel_ready")
        kd_filled = [sem(f"kd_filled{i}") for i in range(BANDS)]
        x_loaded = [sem(f"x_loaded{i}") for i in range(STEPS)]
        out_stored = [sem(f"out_stored{i}") for i in range(STEPS)]
        raw1_done = sem("raw1_done")
        parts1_done = sem("parts1_done")
        stats1_done = sem("stats1_done")
        var1_ready = sem("var1_ready")
        xn1_ready = sem("xn1_ready")
        scores_biased = sem("scores_biased")
        max_done = sem("max_done")
        scores_shifted = sem("scores_shifted")
        sum_done = sem("sum_done")
        inv_ready = sem("inv_ready")
        residual_added = sem("residual_added")
        raw2_done = sem("raw2_done")
        parts2_done = sem("parts2_done")
        stats2_done = sem("stats2_done")
        var2_ready = sem("var2_ready")
        xn2_ready = sem("xn2_ready")
        x2T_split = sem("x2T_split")
        xT_split = sem("xT_split")
        v1_copied = sem("v1_copied")
        out_added = sem("out_added")
        x_biased = sem("x_biased")
        rstd1_ready = sem("rstd1_ready")
        probs_normed = sem("probs_normed")
        rstd2_ready = sem("rstd2_ready")
        x1_biased = sem("x1_biased")
        xT_made = sem("xT_made")
        qk_made = sem("qk_made")
        v_made = sem("v_made")
        o_made = sem("o_made")
        scores_made = sem("scores_made")
        probsT_made = sem("probsT_made")
        proj_made = sem("proj_made")
        x2T_made = sem("x2T_made")
        fc1_made = sem("fc1_made")
        fc2_made = sem("fc2_made")
        xT_copied = sem("xT_copied")
        xT_rounded = sem("xT_rounded")
        qk_copied = sem("qk_copied")
        v0_copied = sem("v0_copied")
        o_copied = sem("o_copied")
        exp_done = sem("exp_done")
        probsT_copied = sem("probsT_copied")
        x2T_copied = sem("x2T_copied")
        gelu_done = sem("gelu_done")
        gelu_loaded = sem("gelu_loaded")

        V_USE, O_USE, Q_USE, K_USE = (0, 2), (1, 5), (3, 6), (4, 7)

        def qkvo_psum(use):
            return psum[:, QKVO_BANK + use % 2, :]

        def scores_psum(band):
            b = psum[:, S_BANK + 2 * band:S_BANK + 2 * band + 2, 0:2 * HEADS * N]
            return b.rearrange("p b (a n) -> p b a n", a=2)

        def tok_psum(use):
            return psum[:, TOK_BANK + use % 2, :]

        PROJ, FC2, XT, X2T, FC1 = 0, 2, 4, 6, 8

        def v_parts(band):
            made = qkvo_psum(V_USE[band]).rearrange("m (a q p d) -> m a q p d", a=PAIRS, q=2, p=2)
            to = vd[:, band, :, :, :, :].rearrange("m (a w) q p d -> m w a q p d", w=2)
            return [(to[HALF * hp:HALF * hp + N, w, :, :, hp, :], made[HALF * w:HALF * w + N, :, :, hp, :])
                    for w in range(2) for hp in range(2)]

        def token_pieces(s, dram, img, tile):
            pieces = []
            for band in range(BANDS):
                row = STEP_ROWS * s + WIN * band + SHIFT
                whole = min(WIN, ROWS - row)
                for first, t0, t1 in ((row, 0, whole), (0, whole, WIN)):
                    if t0 < t1:
                        rows = dram[img, first * COLS:(first + t1 - t0) * COLS, :]
                        pieces.append((rows.rearrange("(t p) c -> p t c", p=COLS),
                                       tile[COLS * band:COLS * (band + 1), t0:t1, :]))
            assert len(pieces) == LOADS[s]
            return pieces

        def dma_count(s, img):
            return img * (16 * LOADS[s]) + 16 * LOADS[s]

        def load_rel(eng, half):
            eng.wait_ge(rel_cleared, 1)
            for ni in range(WIN):
                p, i0 = HALF * half + WIN * ni, WIN - 1 - ni
                eng.dma_start(rel[p:p + WIN, :, :],
                              rel_slices[:, :, i0:i0 + WIN, :].rearrange("q h i j -> q h (i j)")).then_inc(rel_loaded, 16)

        block = ctx.enter_context(nc.Block())

        @block.sync
        def _(sp):
            def load(img, s):
                for src, dst in token_pieces(s, x, img, x_in[:, s, :, :]):
                    sp.dma_start(dst, src).then_inc(x_loaded[s], 16)

            def store(img, s):
                for dst, src in token_pieces(s, out, img, stream[:, s, :, :]):
                    sp.dma_start(dst, src).then_inc(out_stored[s], 16)

            load(0, 0)
            for dst, src in ((wqkv[:, :], w_qkv), (vecs[:, 0:1], g1), (vecs[:, 1:2], b1), (vecs[:, 2:3], g2),
                             (vecs[:, 3:4], b2), (bqkv[:, :], b_qkv), (wproj[:, :], w_proj),
                             (wfc1_raw[:, :], w_fc1), (bfc1[:, :], b_fc1),
                             (wfc2[:, :, :], w_fc2.rearrange("(k p) n -> p k n", p=C)),
                             (brow_proj_in[:, :], b_proj.to_broadcast([TOK, C])),
                             (brow_fc2[:, :], b_fc2.to_broadcast([TOK, C])),
                             (mask_sb[:, :, :, :], mask)):
                sp.dma_start(dst, src).then_inc(weights_loaded, 16)
            load_rel(sp, 0)
            for s in range(1, STEPS):
                load(0, s)

            def fill_kd(at, band):
                wait(sp, qk_copied, at.count(4, 2 * band + 2, 1))
                for h in range(HEADS):
                    rows = slice(HD * h, HD * (h + 1))
                    sp.dma_start(kd[rows, band, h, :], kT[rows, band, :]).then_inc(kd_filled[band], 16)

            def step(at):
                if at.has() and at.has(STEPS):
                    wait(sp, x_biased, at.count(1, 1))
                    load(at.image(STEPS), at.slot())
                if at.has(-2):
                    wait(sp, out_added, at.count(2, 2, -2))
                    store(at.image(-2), at.slot(-2))
                if at.has(1):
                    fill_kd(at, 0)
                    fill_kd(at, 1)

            run_steps(sp, images, step)
            for s in range(STEPS):
                sp.wait_ge(out_stored[s], dma_count(s, images - 1))

        @block.gpsimd
        def _(pool):
            pool.memset(ident[:, :], 0.0).then_inc(ident_zeroed, 1)
            pool.wait_ge(ident_zeroed, 1)
            pool.affine_select(out=ident[:, :], in_=ident[:, :], compare_op=ALU.not_equal, fill=1.0, base=0,
                               pattern=[[-1, 128]], channel_multiplier=1).then_inc(ident_ready, 1)
            pool.memset(minus_half[:, :], -0.5).then_inc(minus_half_ready, 1)
            pool.wait_ge(minus_half_ready, 1)
            pool.wait_ge(weights_loaded, 13 * 16)
            pool.wait_ge(brow_ready, 1)

            def normalise_probs(at, band):
                wait(pool, inv_ready, at.count(2, band + 1))
                p = probs[:, band, :, :, 0:N].rearrange("p a h m -> p (a h) m")
                r = row_inv[:, band, :, :].rearrange("p a h -> p (a h)")
                pool.tensor_tensor(p, p, r.unsqueeze(2).to_broadcast([128, PAIRS * HEADS, N]),
                                   ALU.mult).then_inc(probs_normed, 1)

            def step(at):
                if at.has():
                    normalise_probs(at, 0)
                if at.has(-1):
                    wait(pool, var2_ready, at.count(1, 1, -1))
                    pool.tensor_tensor(rstd2[:, :], ve2[:, :], minus_half[:, :], ALU.pow).then_inc(rstd2_ready, 1)
                    wait(pool, xn2_ready, at.count(2, 2, -1))
                    pool.tensor_tensor(stream[:, at.slot(-1), :, :], stream[:, at.slot(-1), :, :],
                                       brow_fc2[:, :].unsqueeze(1).to_broadcast([TOK, TILES, C]),
                                       ALU.add).then_inc(x1_biased, 1)
                if at.has():
                    normalise_probs(at, 1)
                if at.has(2):
                    wait(pool, var1_ready, at.count(1, 1, 2))
                    pool.tensor_tensor(rstd1[:, :], ve1[:, :], minus_half[:, :], ALU.pow).then_inc(rstd1_ready, 1)
                if at.has(1):
                    wait(pool, x_loaded[at.slot(1)], dma_count(at.slot(1), at.image(1)))
                    wait(pool, xn1_ready, at.count(2, 2, 1))
                    if at.has(1 - STEPS):
                        wait(pool, out_stored[at.slot(1)], dma_count(at.slot(1), at.image(1 - STEPS)))
                    pool.tensor_tensor(stream[:, at.slot(1), :, :], x_in[:, at.slot(1), :, :],
                                       brow_proj[:, :].unsqueeze(1).to_broadcast([TOK, TILES, C]),
                                       ALU.add).then_inc(x_biased, 1)

            run_steps(pool, images, step)

        @block.scalar
        def _(act):
            load_rel(act, 1)
            act.wait_ge(weights_ready, 1)
            act.wait_ge(bias_v_ready, 1)

            def columns_shifted(image, windows, copy):
                last = windows[:, WHOLE, :, :]
                copy(image[:, :, SHIFT:SHIFT + WHOLE * WIN].rearrange("c i (w j) -> c w i j", j=WIN),
                     windows[:, 0:WHOLE, :, :])
                copy(image[:, :, COLS - HEAD:COLS], last[:, :, 0:HEAD])
                return copy(image[:, :, 0:SHIFT], last[:, :, HEAD:WIN])

            def exp(at, band):
                wait(act, scores_shifted, at.count(2, band + 1))
                wait(act, probsT_made, at.count(4, 2 * band + 2, -1))
                act.activation(probs[:, band, :, :, 0:N].rearrange("p a h m -> p (a h) m"),
                               scores[:, band, :, :, :].rearrange("p a h m -> p (a h) m"), ACT.Exp).then_inc(exp_done, 1)

            def copy_probsT(at, band):
                for f in range(2):
                    wait(act, probsT_made, at.count(4, 2 * band + f + 1))
                    act.activation(probsT[:, band, 2 * f:2 * f + 2, :, :].rearrange("p a q n -> p (a q n)"),
                                   psum[:, S_BANK + 2 * band + f, :], ACT.Copy).then_inc(probsT_copied, 1)

            def copy_o(at, band):
                wait(act, o_made, at.count(2, band + 1))
                windows = qkvo_psum(O_USE[band])[:, 0:BAND].rearrange("c (w i j) -> c w i j", i=WIN, j=WIN)
                columns_shifted(oT[:, :, band, :], windows,
                                lambda image, win: act.activation(image, win, ACT.Copy)).then_inc(o_copied, 1)

            def copy_x(at, h):
                t0, t1 = HALVES[h]
                wait(act, xT_made, at.count(2, h + 1, 1))
                for band in range(BANDS):
                    rows = tok_psum(XT + h)[:, 0:(t1 - t0) * TOK].rearrange("c (t b j) -> c t b j", b=BANDS, j=COLS)
                    windows = xT[:, at.slot(1) % 2, band, :, 0:N].rearrange("c w (i j) -> c w i j", j=WIN)
                    last = columns_shifted(rows[:, :, band, :], windows[:, :, t0:t1, :],
                                           lambda image, win: act.activation(win, image, ACT.Copy))
                last.then_inc(xT_copied, 1)

            def round_x(at):
                wait(act, xT_copied, at.count(2, 2, 1))
                act.activation(xT_hi[:, :].rearrange("c (w n) -> c w n", n=N),
                               xT[:, at.slot(1) % 2, 1, :, 0:N], ACT.Copy).then_inc(xT_rounded, 1)

            def copy_x2(at, h):
                t0, t1 = HALVES[h]
                wait(act, x2T_made, at.count(2, h + 1, -1))
                act.activation(x2T_hi[:, t0 * TOK:t1 * TOK], tok_psum(X2T + h)[:, 0:(t1 - t0) * TOK],
                               ACT.Copy).then_inc(x2T_copied, 1)

            def copy_q(at, band):
                wait(act, qk_made, at.count(4, 2 * band + 1, 1))
                act.activation(qT[:, band, :], qkvo_psum(Q_USE[band])[:, 0:BAND], ACT.Identity,
                               bias=bias_q[:, :]).then_inc(qk_copied, 1)

            def copy_k(at, band):
                wait(act, qk_made, at.count(4, 2 * band + 2, 1))
                wait(act, kd_filled[band], at.count(16 * HEADS, 16 * HEADS))
                act.activation(kT[:, band, :], qkvo_psum(K_USE[band])[:, 0:BAND], ACT.Identity,
                               bias=bias_k[:, :]).then_inc(qk_copied, 1)

            def copy_v0(at):
                wait(act, v_made, at.count(2, 1))
                for dst, src in v_parts(0):
                    last = act.activation(dst, src, ACT.Copy)
                last.then_inc(v0_copied, 1)

            def gelu(at, n, d=-1):
                band, chunk = divmod(n, CHUNKS)
                wait(act, fc1_made, at.count(BANDS * CHUNKS, n + 1, d))
                act.activation(hT[:, chunk, band * BAND:(band + 1) * BAND], tok_psum(FC1 + n)[:, 0:BAND],
                               ACT.Gelu, bias=bias_h[:, chunk:chunk + 1]).then_inc(gelu_done, 1)

            def step(at):
                if at.has(-2):
                    gelu(at, 7, -2)
                if at.has():
                    exp(at, 0)
                    copy_v0(at)
                    copy_probsT(at, 0)
                    exp(at, 1)
                if at.has(1):
                    copy_x(at, 0)
                if at.has():
                    copy_o(at, 0)
                if at.has(-1):
                    copy_x2(at, 0)
                if at.has(1):
                    copy_x(at, 1)
                if at.has(-1):
                    wait(act, gelu_loaded, at.count(1, 0, -1))
                    act.activation(table_probe[:, :], bias_h[:, 0:1], ACT.Gelu).then_inc(gelu_loaded, 1)
                    copy_x2(at, 1)
                if at.has(1):
                    copy_q(at, 0)
                if at.has(-1):
                    gelu(at, 0)
                if at.has(1):
                    copy_k(at, 0)
                if at.has(-1):
                    gelu(at, 1)
                if at.has():
                    copy_probsT(at, 1)
                if at.has(1):
                    round_x(at)
                if at.has(-1):
                    gelu(at, 2)
                    gelu(at, 3)
                if at.has():
                    copy_o(at, 1)
                if at.has(1):
                    copy_q(at, 1)
                if at.has(-1):
                    gelu(at, 4)
                if at.has(1):
                    copy_k(at, 1)
                if at.has(-1):
                    gelu(at, 5)
                    gelu(at, 6)

            run_steps(act, images, step)

        @block.vector
        def _(dve):
            dve.memset(rel[:, :, :], 0.0).then_inc(rel_cleared, 1)
            dve.memset(probs[:, :, :, :, :], 0.0)
            dve.memset(kd[:, :, :, :], 0.0)
            dve.memset(xT[:, :, :, :, :].rearrange("c s b w n -> c (s b w) n"), 0.0)
            dve.memset(vd[:, :, :, :, :, :], 0.0)
            dve.memset(psum[:, 0:4, :], 0.0).then_inc(weights_ready, 1)
            dve.wait_ge(weights_loaded, 13 * 16)
            dve.tensor_scalar(wqk[:, 0, :], wqkv[:, 0:C], vecs[:, 0:1], SCALE, ALU.mult, ALU.mult)
            dve.tensor_scalar(wqk[:, 1, :], wqkv[:, C:2 * C], vecs[:, 0:1], None, ALU.mult)
            dve.tensor_scalar(wv[:, :], wqkv[:, 2 * C:3 * C], vecs[:, 0:1], None, ALU.mult)
            dve.tensor_scalar(wfc1[:, :], wfc1_raw[:, :], vecs[:, 2:3], None, ALU.mult).then_inc(weights_scaled, 1)
            dve.wait_ge(weights_scaled, 1)
            dve.tensor_copy(wqk_hi[:, :, :], wqk[:, :, :])
            dve.tensor_copy(wfc1_hi[:, :], wfc1[:, :]).then_inc(weights_scaled, 1)
            dve.wait_ge(weights_scaled, 2)
            dve.tensor_tensor(wqk_lo[:, :, :], wqk[:, :, :], wqk_hi[:, :, :], ALU.subtract)
            dve.tensor_tensor(wfc1_lo[:, :], wfc1[:, :], wfc1_hi[:, :], ALU.subtract).then_inc(weights_ready, 1)
            dve.wait_ge(bias_products, 1)
            made = psum[:, QKVO_BANK, :]
            dve.tensor_scalar(bias_q[:, :], made[:, 0:1], bqkv[:, 0:1], SCALE, ALU.add, ALU.mult)
            dve.tensor_tensor(bias_k[:, :], made[:, 1:2], bqkv[:, 1:2], ALU.add)
            dve.tensor_tensor(bias_v[:, :], made[:, 2:3], bqkv[:, 2:3], ALU.add)
            dve.tensor_tensor(bias_h[:, :], made[:, 3:3 + CHUNKS], bfc1[:, :], ALU.add).then_inc(bias_v_ready, 1)
            dve.wait_ge(bias_v_ready, 1)
            dve.tensor_copy(bias_v_wide[:, :], bias_v[:, 0:1].to_broadcast([C, TOK])).then_inc(bias_v_ready, 1)
            dve.wait_ge(brow_product, 1)
            dve.tensor_tensor(brow_proj[:, :], psum[0:TOK, QKVO_BANK + 1, 0:C], brow_proj_in[:, :],
                              ALU.add).then_inc(brow_ready, 1)

            def make_bias_rel():
                dve.wait_ge(rel_loaded, 2 * WIN * 16)
                for last_band in range(2):
                    for h in range(HEADS):
                        last = dve.tensor_tensor(bias_rel[:, last_band, :, h, :], mask_sb[:, last_band, :, :],
                                                 rel[:, h, :].unsqueeze(1).to_broadcast([128, PAIRS, N]), ALU.add)
                last.then_inc(bias_rel_ready, 1)
                dve.wait_ge(bias_rel_ready, 1)

            def raw_stats(src, raw, t0, t1):
                for t in range(t0, t1):
                    last = dve.bn_stats(raw[:, t, :], src[:, t, :])
                return last

            def mean_var(raw, part, mean, ve, raw_done, parts_done, stats_done, ready, n):
                mean0, mean1 = raw[:, :, 1], raw[:, :, 4]
                wait(dve, raw_done, n)
                dve.tensor_tensor(part[:, 0, :], mean0, mean1, ALU.add)
                dve.tensor_tensor(part[:, 1, :], mean0, mean1, ALU.subtract)
                dve.scalar_tensor_tensor(part[:, 2, :], raw[:, :, 2], C * EPS, raw[:, :, 5], ALU.add,
                                         ALU.add).then_inc(parts_done, 1)
                wait(dve, parts_done, n)
                dve.tensor_scalar(mean[:, :], part[:, 0, :], 0.5, None, ALU.mult)
                dve.scalar_tensor_tensor(part[:, 3, :], part[:, 1, :], 0.25, part[:, 1, :], ALU.mult,
                                         ALU.mult).then_inc(stats_done, 1)
                wait(dve, stats_done, n)
                dve.scalar_tensor_tensor(ve[:, :], part[:, 2, :], 1.0 / C, part[:, 3, :], ALU.mult,
                                         ALU.add).then_inc(ready, 1)

            def normalise(dst, src, mean, rstd, ready):
                for t0, t1 in HALVES:
                    for t in range(t0, t1):
                        last = dve.tensor_scalar(dst[:, t, :], src[:, t, :], mean[:, t:t + 1], rstd[:, t:t + 1],
                                                 ALU.subtract, ALU.mult)
                    last.then_inc(ready, 1)

            def shift_scores(at, band):
                sc = scores[:, band, :, :, :].rearrange("p (b a) h m -> p b (a h m)", b=2)
                rows = scores[:, band, :, :, :].rearrange("p a h m -> p (a h) m")
                mx = row_max[:, band, :, :].rearrange("p a h -> p (a h)")
                last_band = int(at.s == STEPS - 1 and band == BANDS - 1)
                wait(dve, scores_made, at.count(2, band + 1))
                wait(dve, exp_done, at.count(2, band + 1, -1))
                dve.tensor_tensor(sc, scores_psum(band).rearrange("p b a n -> p b (a n)"),
                                  bias_rel[:, last_band, :, :, :].rearrange("p (b a) h m -> p b (a h m)", b=2),
                                  ALU.add).then_inc(scores_biased, 1)
                wait(dve, scores_biased, at.count(2, band + 1))
                dve.tensor_reduce(mx, rows, AX_X, ALU.max).then_inc(max_done, 1)
                wait(dve, max_done, at.count(2, band + 1))
                dve.tensor_tensor(rows, rows, mx.unsqueeze(2).to_broadcast([128, HEADS * PAIRS, N]),
                                  ALU.subtract).then_inc(scores_shifted, 1)

            def inverse_sums(at, band):
                p = probs[:, band, :, :, 0:N].rearrange("p a h m -> p (a h) m")
                s = row_sum[:, band, :, :].rearrange("p a h -> p (a h)")
                r = row_inv[:, band, :, :].rearrange("p a h -> p (a h)")
                wait(dve, exp_done, at.count(2, band + 1))
                dve.tensor_reduce(s, p, AX_X, ALU.add).then_inc(sum_done, 1)
                wait(dve, sum_done, at.count(2, band + 1))
                dve.reciprocal(r, s).then_inc(inv_ready, 1)

            def add_to_stream(slot, use, h):
                t0, t1 = HALVES[h]
                s = stream[:, slot, t0:t1, :].rearrange("p t c -> p (t c)")
                return dve.tensor_tensor(s, tok_psum(use)[0:TOK, 0:(t1 - t0) * C], s, ALU.add)

            def copy_v1(at):
                wait(dve, v_made, at.count(2, 2))
                for dst, src in v_parts(1):
                    last = dve.tensor_copy(dst, src)
                last.then_inc(v1_copied, 1)

            def split_x(at):
                wait(dve, xT_rounded, at.count(1, 1, 1))
                dve.tensor_tensor(xT_lo[:, :].rearrange("c (w n) -> c w n", n=N),
                                  xT[:, at.slot(1) % 2, 1, :, 0:N],
                                  xT_hi[:, :].rearrange("c (w n) -> c w n", n=N),
                                  ALU.subtract).then_inc(xT_split, 1)

            def split_x2(at, h):
                t0, t1 = HALVES[h]
                wait(dve, x2T_copied, at.count(2, h + 1, -1))
                dve.tensor_tensor(x2T_lo[:, t0 * TOK:t1 * TOK], tok_psum(X2T + h)[:, 0:(t1 - t0) * TOK],
                                  x2T_hi[:, t0 * TOK:t1 * TOK], ALU.subtract).then_inc(x2T_split, 1)

            def add_mlp(at, h):
                wait(dve, x1_biased, at.count(1, 1, -2))
                wait(dve, fc2_made, at.count(2, h + 1, -2))
                add_to_stream(at.slot(-2), FC2 + h, h).then_inc(out_added, 1)

            def step(at):
                if at.has() and not at.has(-1):
                    make_bias_rel()
                if at.has():
                    shift_scores(at, 0)
                if at.has(-1):
                    wait(dve, x_biased, at.count(1, 1, -1))
                    for h in range(2):
                        wait(dve, proj_made, at.count(2, h + 1, -1))
                        add_to_stream(at.slot(-1), PROJ + h, h).then_inc(residual_added, 1)
                if at.has():
                    inverse_sums(at, 0)
                if at.has(-1):
                    wait(dve, xn2_ready, at.count(2, 2, -2))
                    for h, (t0, t1) in enumerate(HALVES):
                        wait(dve, residual_added, at.count(2, h + 1, -1))
                        last = raw_stats(stream[:, at.slot(-1), :, :], raw2, t0, t1)
                    last.then_inc(raw2_done, 1)
                    mean_var(raw2, part2, mean2, ve2, raw2_done, parts2_done, stats2_done, var2_ready,
                             at.count(1, 1, -1))
                if at.has():
                    shift_scores(at, 1)
                if at.has(-2):
                    add_mlp(at, 0)
                if at.has(-1):
                    wait(dve, rstd2_ready, at.count(1, 1, -1))
                    wait(dve, x2T_made, at.count(2, 2, -2))
                    normalise(xn2, stream[:, at.slot(-1), :, :], mean2, rstd2, xn2_ready)
                if at.has(-2):
                    add_mlp(at, 1)
                if at.has():
                    inverse_sums(at, 1)
                if at.has(-1):
                    split_x2(at, 0)
                if at.has():
                    copy_v1(at)
                if at.has(-1):
                    split_x2(at, 1)
                if at.has(2):
                    wait(dve, x_loaded[at.slot(2)], dma_count(at.slot(2), at.image(2)))
                    wait(dve, xn1_ready, at.count(2, 2, 1))
                    raw_stats(x_in[:, at.slot(2), :, :], raw1, 0, TILES).then_inc(raw1_done, 1)
                    mean_var(raw1, part1, mean1, ve1, raw1_done, parts1_done, stats1_done, var1_ready,
                             at.count(1, 1, 2))
                if at.has(1):
                    split_x(at)
                if at.has(2):
                    wait(dve, rstd1_ready, at.count(1, 1, 2))
                    wait(dve, xT_made, at.count(2, 2, 1))
                    normalise(xn1, x_in[:, at.slot(2), :, :], mean1, rstd1, xn1_ready)

            run_steps(dve, images, step)

        @block.tensor
        def _(pe):
            pe.wait_ge(weights_loaded, 13 * 16)
            for k in range(3):
                pe.matmul(psum[:, QKVO_BANK, k:k + 1], wqkv[:, k * C:(k + 1) * C], vecs[:, 1:2],
                          start=True, stop=True)
            for k in range(CHUNKS):
                last = pe.matmul(psum[:, QKVO_BANK, 3 + k:4 + k], wfc1_raw[:, k * C:(k + 1) * C], vecs[:, 3:4],
                                 start=True, stop=True)
            last.then_inc(bias_products, 1)
            pe.wait_ge(bias_v_ready, 2)
            pe.matmul(psum[0:TOK, QKVO_BANK + 1, 0:C], bias_v_wide[:, :], wproj[:, :], start=True,
                      stop=True).then_inc(brow_product, 1)
            pe.wait_ge(weights_ready, 2)
            pe.wait_ge(ident_ready, 1)

            def make_scores(band):
                for w in range(WINDOWS):
                    half, pair = HALF * (w % 2), w // 2
                    cols = slice(w * N, (w + 1) * N)
                    last = pe.matmul(scores_psum(band)[half:half + N, pair // 2, pair % 2, :],
                                     qT[:, band, cols], kd[:, band, :, cols], start=True, stop=True)
                last.then_inc(scores_made, 1)

            def transpose_tiles(src, use, h):
                t0, t1 = HALVES[h]
                for t in range(t0, t1):
                    last = pe.transpose(tok_psum(use)[:, (t - t0) * TOK:(t - t0 + 1) * TOK], src[:, t, :],
                                        ident[0:TOK, 0:TOK])
                return last

            def transpose_probs(at, band):
                wait(pe, probs_normed, at.count(2, band + 1))
                for f in range(2):
                    for n in range(4):
                        pair, hq = 2 * f + n // 2, n % 2
                        last = pe.transpose(psum[:, S_BANK + 2 * band + f, 128 * n:128 * (n + 1)],
                                            probs[:, band, pair, 2 * hq:2 * hq + 2, :].rearrange("p h m -> p (h m)"),
                                            ident[:, :])
                    last.then_inc(probsT_made, 1)

            def attend(at, band):
                wait(pe, probsT_copied, at.count(4, 2 * band + 2))
                wait(pe, (v0_copied, v1_copied)[band], at.count(1, 1))
                if band == 0:
                    wait(pe, qk_copied, at.count(4, 4))
                elif at.has(1):
                    wait(pe, qk_copied, at.count(4, 1, 1))
                for w in range(WINDOWS):
                    for hq in range(2):
                        last = pe.matmul(qkvo_psum(O_USE[band])[HALF * hq:HALF * (hq + 1), w * N:(w + 1) * N],
                                         vd[:, band, w, hq, :, :].rearrange("m p d -> m (p d)"),
                                         probsT[:, band, w // 2, hq, HALF * (w % 2):HALF * (w % 2) + N],
                                         start=True, stop=True)
                last.then_inc(o_made, 1)

            def product(made, w_hi, w_lo, x_hi, x_lo):
                pe.matmul(made, w_hi, x_hi, start=True, stop=False)
                pe.matmul(made, w_lo, x_hi, start=False, stop=False)
                return pe.matmul(made, w_hi, x_lo, start=False, stop=True)

            def qk_product(at, use, part, band):
                if band == 0:
                    return pe.matmul(qkvo_psum(use)[:, 0:BAND], wqk[:, part, :], xT[:, at.slot(1) % 2, 0, :, 0:N],
                                     start=True, stop=True)
                return product(qkvo_psum(use)[:, 0:BAND], wqk_hi[:, part, :], wqk_lo[:, part, :],
                               xT_hi[:, :], xT_lo[:, :])

            def make_q(at, band):
                if band == 0:
                    wait(pe, xT_copied, at.count(2, 2, 1))
                else:
                    wait(pe, xT_split, at.count(1, 1, 1))
                if band == 0:
                    wait(pe, o_copied, at.count(2, 1))
                else:
                    wait(pe, qk_copied, at.count(4, 2, 1))
                qk_product(at, Q_USE[band], 0, band).then_inc(qk_made, 1)

            def make_k(at, band):
                if band == 0:
                    wait(pe, v1_copied, at.count(1, 1))
                else:
                    wait(pe, o_copied, at.count(2, 2))
                qk_product(at, K_USE[band], 1, band).then_inc(qk_made, 1)

            def make_values(at, band):
                if band == 0:
                    wait(pe, qk_copied, at.count(4, 3))
                else:
                    wait(pe, v0_copied, at.count(1, 1))
                rows = HALF + N
                for pair in range(PAIRS):
                    windows = xT[:, at.slot() % 2, band, 2 * pair:2 * pair + 2, :].rearrange("c w n -> c (w n)")
                    last = pe.matmul(qkvo_psum(V_USE[band])[0:rows, pair * C:(pair + 1) * C], windows[:, 0:rows],
                                     wv[:, :], start=True, stop=True)
                last.then_inc(v_made, 1)

            def project(at, h):
                wait(pe, gelu_done, at.count(BANDS * CHUNKS, BANDS * CHUNKS - 1 + h, -2))
                t0, t1 = HALVES[h]
                for t in range(t0, t1):
                    last = pe.matmul(tok_psum(PROJ + h)[0:TOK, (t - t0) * C:(t - t0 + 1) * C],
                                     oT[:, t, :, :].rearrange("c b j -> c (b j)"), wproj[:, :], start=True, stop=True)
                last.then_inc(proj_made, 1)

            def transpose_x(at, h):
                wait(pe, xn1_ready, at.count(2, h + 1, 1))
                if at.has(-2):
                    wait(pe, out_added, at.count(2, h + 1, -2))
                else:
                    wait(pe, residual_added, at.count(2, h + 1, -1))
                transpose_tiles(xn1, XT + h, h).then_inc(xT_made, 1)

            def transpose_x2(at, h):
                wait(pe, xn2_ready, at.count(2, h + 1, -1))
                if at.has(1):
                    wait(pe, xT_copied, at.count(2, h + 1, 1))
                else:
                    wait(pe, out_added, at.count(2, h + 1, -2))
                transpose_tiles(xn2, X2T + h, h).then_inc(x2T_made, 1)

            def make_hidden(at, n, d=-1):
                band, chunk = divmod(n, CHUNKS)
                if n < 2:
                    wait(pe, x2T_split, at.count(2, n + 1, -1))
                else:
                    wait(pe, gelu_done, at.count(BANDS * CHUNKS, n - 1, d))
                rows, cols = slice(band * BAND, (band + 1) * BAND), slice(chunk * C, (chunk + 1) * C)
                product(tok_psum(FC1 + n)[:, 0:BAND], wfc1_hi[:, cols], wfc1_lo[:, cols], x2T_hi[:, rows],
                        x2T_lo[:, rows]).then_inc(fc1_made, 1)

            def make_out(at, h):
                if at.has(-1):
                    wait(pe, residual_added, at.count(2, h + 1, -1))
                t0, t1 = HALVES[h]
                for t in range(t0, t1):
                    for chunk in range(CHUNKS):
                        last = pe.matmul(tok_psum(FC2 + h)[0:TOK, (t - t0) * C:(t - t0 + 1) * C],
                                         hT[:, chunk, t * TOK:(t + 1) * TOK], wfc2[:, chunk, :],
                                         start=chunk == 0, stop=chunk == CHUNKS - 1)
                last.then_inc(fc2_made, 1)

            def scores(at, band):
                wait(pe, kd_filled[band], at.count(16 * HEADS, 16 * HEADS))
                wait(pe, probsT_copied, at.count(4, 2 * band + 2, -1))
                make_scores(band)

            def step(at):
                if at.has():
                    scores(at, 0)
                if at.has(-2):
                    make_hidden(at, 7, -2)
                if at.has(-1):
                    wait(pe, o_copied, at.count(2, 2, -1))
                    project(at, 0)
                    project(at, 1)
                if at.has():
                    make_values(at, 0)
                    scores(at, 1)
                if at.has(-2):
                    wait(pe, gelu_done, at.count(BANDS * CHUNKS, BANDS * CHUNKS, -2))
                    make_out(at, 0)
                if at.has():
                    transpose_probs(at, 0)
                if at.has(-2):
                    make_out(at, 1)
                if at.has(1):
                    transpose_x(at, 0)
                if at.has():
                    attend(at, 0)
                if at.has(-1):
                    transpose_x2(at, 0)
                if at.has(1):
                    transpose_x(at, 1)
                if at.has():
                    make_values(at, 1)
                if at.has(-1):
                    transpose_x2(at, 1)
                if at.has(1):
                    make_q(at, 0)
                if at.has(-1):
                    make_hidden(at, 0)
                if at.has(1):
                    make_k(at, 0)
                if at.has(-1):
                    make_hidden(at, 1)
                if at.has():
                    transpose_probs(at, 1)
                if at.has(-1):
                    make_hidden(at, 2)
                    make_hidden(at, 3)
                if at.has():
                    attend(at, 1)
                if at.has(1):
                    make_q(at, 1)
                if at.has(-1):
                    make_hidden(at, 4)
                if at.has(1):
                    make_k(at, 1)
                if at.has(-1):
                    make_hidden(at, 5)
                    make_hidden(at, 6)

            run_steps(pe, images, step)


def window_mask():
    part = np.zeros((2, WIN), np.int64)
    part[1, WIN - SHIFT:] = 1
    full = np.zeros((128, 2, PAIRS, N), np.float32)
    for last_band in range(2):
        for w in range(WINDOWS):
            region = (2 * part[last_band][:, None] + part[int(w == WINDOWS - 1)][None, :]).reshape(-1)
            differ = region[:, None] != region[None, :]
            p0 = HALF * (w % 2)
            full[p0:p0 + N, last_band, w // 2, :] = np.where(differ, -100.0, 0.0)
    return full


def kernel(x, L0_conv_g1, L0_conv_b1, L0_conv_w_qkv, L0_conv_b_qkv, L0_conv_w_proj, L0_conv_b_proj,
           L0_conv_rel_table, L0_conv_g2, L0_conv_b2, L0_conv_w_fc1, L0_conv_b_fc1, L0_conv_w_fc2,
           L0_conv_b_fc2):
    import concourse.bacc as bacc
    from concourse.bass_utils import run_bass_kernel_spmd

    x = np.asarray(x)
    shape = x.shape
    span = 2 * WIN - 1
    flipped = np.asarray(L0_conv_rel_table).reshape(span, span, HEADS)[::-1, ::-1].transpose(2, 0, 1)
    laid = {
        "x": x.reshape(shape[0], IMG, C),
        "g1": np.asarray(L0_conv_g1).reshape(C, 1),
        "b1": np.asarray(L0_conv_b1).reshape(C, 1),
        "w_qkv": np.asarray(L0_conv_w_qkv),
        "b_qkv": np.asarray(L0_conv_b_qkv).reshape(3, C).T,
        "w_proj": np.asarray(L0_conv_w_proj),
        "b_proj": np.asarray(L0_conv_b_proj).reshape(1, C),
        "rel_slices": np.stack([flipped[:, :, WIN - 1 - nj:2 * WIN - 1 - nj] for nj in range(WIN)]),
        "g2": np.asarray(L0_conv_g2).reshape(C, 1),
        "b2": np.asarray(L0_conv_b2).reshape(C, 1),
        "w_fc1": np.asarray(L0_conv_w_fc1),
        "b_fc1": np.asarray(L0_conv_b_fc1).reshape(CHUNKS, C).T,
        "w_fc2": np.asarray(L0_conv_w_fc2),
        "b_fc2": np.asarray(L0_conv_b_fc2).reshape(1, C),
        "mask": window_mask(),
    }
    nc = bacc.Bacc("TRN2", target_bir_lowering=False, num_devices=1)
    arrays, aps = {}, []
    for name, a in laid.items():
        arrays[f"in_{name}"] = np.ascontiguousarray(a)
        aps.append(nc.dram_tensor(f"in_{name}", a.shape, F32, kind="ExternalInput").ap())
    aps.append(nc.dram_tensor("out", (shape[0], IMG, C), F32, kind="ExternalOutput").ap())
    swin_block(nc, *aps)
    r = run_bass_kernel_spmd(nc, [arrays], core_ids=[0])
    return r.results[0]["out"].reshape(shape)
```
